# Optimizing a Trainium2 kernel written in Bass

```python
import numpy as np
import jax
import jax.numpy as jnp

def _softmax(x, axis=-1):
    return jax.nn.softmax(x, axis=axis)

def _gelu(x):
    return jax.nn.gelu(x, approximate=True)

def _silu(x):
    return jax.nn.silu(x)

def _sigmoid(x):
    return jax.nn.sigmoid(x)

def _layernorm(x, axis=-1, eps=1e-05):
    m = jnp.mean(x, axis=axis, keepdims=True)
    v = jnp.var(x, axis=axis, keepdims=True)
    return (x - m) / jnp.sqrt(v + eps)

def _scatter_add(tgt, idx, src, axis=0):
    return tgt.at[idx].add(src)

def _segment_sum(src, seg, n):
    return jax.ops.segment_sum(src, seg, n)
kernel_name = 'mk_recurrent_d1_jaxref_r8_c8ed87'

def setup_inputs(seed: int=0):
    np.random.seed(seed)
    _w = jnp.asarray

    def _L0_attn_setup():
        import jax, jax.numpy as jnp
        import numpy as np
        EMBED = 512
        H = 32
        KV = 8
        D = EMBED // H
        REP = H // KV

        def _rope(t, cos, sin):
            t = t.reshape(*t.shape[:-1], 2, D // 2)
            t1, t2 = (t[..., 0, :], t[..., 1, :])
            return jnp.concatenate([t1 * cos - t2 * sin, t1 * sin + t2 * cos], axis=-1)
        key = jax.random.key(seed)
        ks = jax.random.split(key, 7)
        B, S = (1, 256)
        x = jax.random.normal(ks[0], (B, S, EMBED), dtype=jnp.float32)
        wq = jax.random.normal(ks[1], (EMBED, EMBED), dtype=jnp.float32) * 0.02
        bq = jax.random.normal(ks[2], (EMBED,), dtype=jnp.float32) * 0.02
        wk = jax.random.normal(ks[3], (EMBED, KV * D), dtype=jnp.float32) * 0.02
        bk = jax.random.normal(ks[4], (KV * D,), dtype=jnp.float32) * 0.02
        wv = jax.random.normal(ks[5], (EMBED, KV * D), dtype=jnp.float32) * 0.02
        bv = jax.random.normal(ks[6], (KV * D,), dtype=jnp.float32) * 0.02
        return {'x': x, 'wq': wq, 'bq': bq, 'wk': wk, 'bk': bk, 'wv': wv, 'bv': bv}
    _L0_attn_in = _L0_attn_setup()

    def _L0_ffn_setup():
        import jax, jax.numpy as jnp
        import numpy as np
        C_CLAMP = 0.5
        EPS = 1e-06
        key = jax.random.key(seed)
        ks = jax.random.split(key, 6)
        B_, S, D, O, R, E = (4, 256, 512, 512, 16, 8)
        x = jax.random.normal(ks[0], (B_, S, D), dtype=jnp.float32)
        W = jax.random.normal(ks[1], (O, D), dtype=jnp.float32) * (1.0 / np.sqrt(D))
        b = jax.random.normal(ks[2], (O,), dtype=jnp.float32) * 0.01
        A = jax.random.normal(ks[3], (E, D, R), dtype=jnp.float32) * (1.0 / np.sqrt(D))
        Bm = jax.random.normal(ks[4], (E, R, O), dtype=jnp.float32) * (1.0 / np.sqrt(R))
        p_scores = jax.random.uniform(ks[5], (E,), dtype=jnp.float32)
        return {'x': x, 'W': W, 'b': b, 'A': A, 'B': Bm, 'p_scores': p_scores}
    _L0_ffn_in = _L0_ffn_setup()
    _d = {'L0_attn_x': _L0_attn_in['x'], 'L0_attn_wq': _L0_attn_in['wq'], 'L0_attn_bq': _L0_attn_in['bq'], 'L0_attn_wk': _L0_attn_in['wk'], 'L0_attn_bk': _L0_attn_in['bk'], 'L0_attn_wv': _L0_attn_in['wv'], 'L0_attn_bv': _L0_attn_in['bv'], 'L0_ffn_W': _L0_ffn_in['W'], 'L0_ffn_b': _L0_ffn_in['b'], 'L0_ffn_A': _L0_ffn_in['A'], 'L0_ffn_B': _L0_ffn_in['B'], 'L0_ffn_p_scores': _L0_ffn_in['p_scores']}
    _x0 = _d['L0_attn_x']
    _d['L0_attn_x'] = jax.random.normal(jax.random.fold_in(jax.random.key(seed), 1), (1, 1024, 512), dtype=_x0.dtype)
    del _x0
    return _d

def reference(L0_attn_x, L0_attn_wq, L0_attn_bq, L0_attn_wk, L0_attn_bk, L0_attn_wv, L0_attn_bv, L0_ffn_W, L0_ffn_b, L0_ffn_A, L0_ffn_B, L0_ffn_p_scores):

    def _L0_attn_ref(x, wq, bq, wk, bk, wv, bv):
        import jax, jax.numpy as jnp
        import numpy as np
        EMBED = 512
        H = 32
        KV = 8
        D = EMBED // H
        REP = H // KV

        def _rope(t, cos, sin):
            t = t.reshape(*t.shape[:-1], 2, D // 2)
            t1, t2 = (t[..., 0, :], t[..., 1, :])
            return jnp.concatenate([t1 * cos - t2 * sin, t1 * sin + t2 * cos], axis=-1)
        B, S, E = x.shape
        xq = (x @ wq + bq).reshape(B, S, H, D)
        xk = (x @ wk + bk).reshape(B, S, KV, D)
        xv = (x @ wv + bv).reshape(B, S, KV, D)
        inv_freq = 1.0 / 10000.0 ** (jnp.arange(0, D, 2, dtype=jnp.float32) / D)
        ang = jnp.arange(S, dtype=jnp.float32)[:, None] * inv_freq[None, :]
        cos, sin = (jnp.cos(ang)[:, None, :], jnp.sin(ang)[:, None, :])
        q = _rope(xq, cos, sin)
        k = _rope(xk, cos, sin)
        k = jnp.repeat(k, REP, axis=2)
        v = jnp.repeat(xv, REP, axis=2)
        scores = jnp.einsum('bqhd,bkhd->bhqk', q, k) / jnp.sqrt(jnp.float32(D))
        probs = jax.nn.softmax(scores.astype(jnp.float32), axis=-1)
        out = jnp.einsum('bhqk,bkhd->bqhd', probs, v).reshape(B, S, E)
        return out

    def _L0_ffn_ref(x, W, b, A, B, p_scores):
        import jax, jax.numpy as jnp
        import numpy as np
        C_CLAMP = 0.5
        EPS = 1e-06
        z = jnp.einsum('bsd,od->bso', x, W) + b
        u = jnp.einsum('bsd,edr->ebsr', x, A)
        m = jnp.einsum('ebsr,ero,e->bso', u, B, p_scores)
        norm_z = jnp.linalg.norm(z, axis=-1, keepdims=True)
        norm_m = jnp.linalg.norm(m, axis=-1, keepdims=True)
        gamma = jnp.minimum(C_CLAMP * norm_z / (norm_m + EPS), 1.0)
        return z + gamma * m
    x = L0_attn_x
    xn = _layernorm(x, axis=-1)
    s = _L0_attn_ref(xn, L0_attn_wq, L0_attn_bq, L0_attn_wk, L0_attn_bk, L0_attn_wv, L0_attn_bv)
    g = _silu(_L0_ffn_ref(xn, L0_ffn_W, L0_ffn_b, L0_ffn_A, L0_ffn_B, L0_ffn_p_scores))
    x = x + s * g
    return x

_drawn_inputs = setup_inputs


def setup_inputs(seed=0):
    import zlib

    import numpy as np

    out = dict(_drawn_inputs(seed))
    spreads = {}
    factors = {'L0_attn_wq': 8.0,
     'L0_attn_bq': 8.0,
     'L0_attn_wk': 8.0,
     'L0_attn_bk': 8.0,
     'L0_attn_wv': 4.183,
     'L0_ffn_W': 2.852,
     'L0_ffn_b': 25.559,
     'L0_ffn_A': 5.79,
     'L0_ffn_B': 5.755,
     'L0_ffn_p_scores': 8.0,
     'L0_attn_bv': 4.493}
    for name, (base, spread) in spreads.items():
        noise = np.random.default_rng([zlib.crc32(name.encode()), seed]).standard_normal(out[name].shape)
        drawn = base * np.exp(spread * noise) if base else spread * noise
        out[name] = jnp.asarray(drawn.astype(out[name].dtype))
    for name, factor in factors.items():
        out[name] = (out[name] * factor).astype(out[name].dtype)
    return out
```

```python
from contextlib import ExitStack

import numpy as np

import concourse.bass as bass
from concourse import mybir
from concourse.alu_op_type import AluOpType as ALU

F32 = mybir.dt.float32
BF16 = mybir.dt.bfloat16
ACT = mybir.ActivationFunctionType
AX = mybir.AxisListType

P = 128
S = 1024
E = 512
H, KV = 32, 8
D = E // H
REP = H // KV
NT = S // P
NE = E // P
HALF = S // 2
TH = NT // 2
CHUNKS = H // KV
RANK = 128
PARTS = 3
Q_SLOTS = (0, 1, 0, 1, 0, 2)
K_SLOTS = (0, 0, 1, 1, 2, 0)
KR = D * len(Q_SLOTS)
KM = KR + 2
VC = 32
PB = 4
ROW_ORDER = [j // 2 + (D // 2) * (j % 2) for j in range(D)]
PARTNER = [i ^ 8 for i in range(32)]
C_CLAMP, EPS_LN, EPS_M = 0.5, 1e-5, 1e-6

PJ = ([("xT", t, "act") for t in range(NT)]
      + [("k", hh, "dve") for hh in range(2)]
      + [("q", (0, hh), "dve") for hh in range(2)]
      + [("v", hh, "dve") for hh in range(2)]
      + [("q", (c, hh), "dve") for c in range(1, CHUNKS) for hh in range(2)]
      + [("u", hh, "act") for hh in range(2)])
for _t in range(NT):
    PJ += [("z", _t, "dve"), ("m", _t, "act")]
    if _t == 5:
        PJ += [("max0", 0, "act")]
PJ_AT = {(kind, i): n for n, (kind, i, _) in enumerate(PJ)}


def emptied(n):
    who = PJ[n][2]
    return who, sum(w == who for _, _, w in PJ[:n + 1])


ST_PER, SM_PER = 66, 34
MAX1_SLOT, MAX0_SLOT = 2, 10
OUT1_SLOT, OUT0_SLOT = 2, 10


def st_score(g, s, h):
    return ST_PER * g + 4 * s + h + (s >= MAX1_SLOT) + (s >= MAX0_SLOT)


def st_max1(g):
    return ST_PER * g + 4 * MAX1_SLOT


def st_max0(g):
    return ST_PER * g + 4 * MAX0_SLOT + 1


def sm_base(g):
    return 31 + SM_PER * g


def sm_score(g, e, first=False):
    return sm_base(g) + e + (1 if e >= 2 * OUT1_SLOT else 0) + (1 if e >= 2 * OUT0_SLOT else 0) \
        + (1 if first and e < 2 * OUT1_SLOT else 0)


def sm_out1(g):
    return sm_base(g) + 2 * OUT1_SLOT


def sm_out0(g):
    return sm_base(g) + 2 * OUT0_SLOT + 1


LAST = KV - 1
SM_LAST_OUT1 = sm_base(LAST)
SM_LAST_OUT0 = SM_LAST_OUT1 + 1
SM_TAIL_OUT1 = SM_LAST_OUT1 + 2


def build(nc, x, wq, wk, wv, biases, bv, wT, b, A, B, p_sc, cosT, sinT, ident, identb, ones, out):
    ctx = ExitStack()
    with ctx:
        def sb(name, shape, dt=F32):
            return ctx.enter_context(nc.sbuf_tensor(name, shape, dt))

        def sem(name):
            return ctx.enter_context(nc.semaphore(name))

        x_sb = sb("x_sb", [P, NT, E])
        arena = sb("arena", [P, PB, REP, HALF])
        flat = arena[:, :, :, :].rearrange("p a b c -> p (a b c)")
        xT = flat[:, 0:NE * S].rearrange("p (c n) -> p c n", c=NE)
        wq_sb = flat[:, NE * S:NE * S + NE * E].rearrange("p (c n) -> p c n", c=NE)
        wT_sb = flat[:, NE * S + NE * E:NE * S + 2 * NE * E].rearrange("p (c n) -> p c n", c=NE)
        probs = arena
        xn = sb("xn", [P, 2, E])
        wk_sb = sb("wk_sb", [P, NE, P])
        wv_sb = sb("wv_sb", [P, NE, P])
        A_sb = sb("A_sb", [P, NE, RANK])
        B_sb = sb("B_sb", [RANK, E])
        tables = sb("tables", [P, 2, S])
        cos_sb, sin_sb = tables[:, 0, :], tables[:, 1, :]
        heads = tables[:, 0, :].rearrange("p (a n) -> p a n", a=2)
        gated = tables[:, 1, 0:TH * REP * D].rearrange("p (t n) -> p t n", t=TH)
        uT = sb("uT", [RANK, S])
        rot = sb("rot", [P, 2, HALF])
        swp = sb("swp", [P, 2, HALF])
        parts = sb("parts", [P, 3, PARTS, HALF], BF16)
        qA = sb("qA", [KM, 2, KV, REP, HALF], BF16)
        kA = sb("kA", [KM, KV, S], BF16)
        z_sb = sb("z_sb", [P, NT, E])
        m_sb = sb("m_sb", [P, 3, E])
        junk = sb("junk", [P, 2, E], BF16)
        v_sb = sb("v_sb", [P, NT, KV * D])
        vg = sb("vg", [P, NT, VC])
        id_sb = sb("id_sb", [P, P])
        idb_sb = sb("idb_sb", [P, P], BF16)
        b_sb = sb("b_sb", [P, E])
        bv_sb = sb("bv_sb", [P, KV * D])
        bias = sb("bias", [P, CHUNKS + 1, 2])
        p_sb = sb("p_sb", [RANK, 1])
        stats = sb("stats", [P, NT, 6])
        mv = sb("mv", [P, NT, 2])
        rstd = sb("rstd", [P, NT])
        consts = sb("consts", [P, 4])
        norms = sb("norms", [P, NT, 2])
        gam = sb("gam", [P, NT, 2])
        negmax = sb("negmax", [P, 2, 16])
        maxp = sb("maxp", [P, 2, 32], BF16)
        maxT = sb("maxT", [32, 2, P], BF16)
        rsum = sb("rsum", [P, TH * REP])
        scaled = sb("scaled", [P, TH, REP * D])

        sm = ctx.enter_context(nc.psum_tensor("sm", [P, 2, S], F32))
        st = ctx.enter_context(nc.psum_tensor("st", [P, 3, HALF], F32))
        oT = ctx.enter_context(nc.psum_tensor("oT", [P, HALF], F32))

        def pj(n):
            return oT[:, :] if n % 4 == 3 else st[:, n % 4, :]

        x_in = [sem(f"x_in{t}") for t in range(NT)]
        wk_in, wq0_in, wq_in, wv_in, tab_in, ffn_in, small_in = (sem(n) for n in (
            "wk_in", "wq0_in", "wq_in", "wv_in", "tab_in", "ffn_in", "small_in"))
        ones_in = sem("ones_in")
        const_set = sem("const_set")
        stats_done, mean_var, eps_added, rstd_done = (sem(n) for n in (
            "stats_done", "mean_var", "eps_added", "rstd_done"))
        xn_done = sem("xn_done")
        pj_full, pj_act, pj_dve = sem("pj_full"), sem("pj_act"), sem("pj_dve")
        cos_mul, swapped, sin_mul = sem("cos_mul"), sem("swapped"), sem("sin_mul")
        rotated, part1, left1, part2, part3 = (sem(n) for n in ("rotated", "part1", "left1", "part2", "part3"))
        stacked = [sem(f"stacked{n}") for n in range(2 + 2 * CHUNKS)]
        norm_done, pow_step, gamma_done = sem("norm_done"), sem("pow_step"), sem("gamma_done")
        gate_in, gate_exp, exp_plus1, gate_sig, gate_done = (sem(n) for n in (
            "gate_in", "gate_exp", "exp_plus1", "gate_sig", "gate_done"))
        sm_full, sm_free = sem("sm_full"), sem("sm_free")
        st_full, st_free = sem("st_full"), sem("st_free")
        max_hi, max_parts, max_in = sem("max_hi"), sem("max_parts"), sem("max_in")
        v_ready, pv_done = sem("v_ready"), sem("pv_done")
        heads_out, sums_inv, heads_scaled, heads_gated, group_done = (sem(n) for n in (
            "heads_out", "sums_inv", "heads_scaled", "heads_gated", "group_done"))
        stored = sem("stored")

        halves = [("k", hh) for hh in range(2)] + [("q", (c, hh)) for c in range(CHUNKS) for hh in range(2)]
        block = ctx.enter_context(nc.Block())

        @block.sync
        def _(sp):
            for t in range(NT):
                sp.dma_start(x_sb[:, t, :], x[t * P:(t + 1) * P, :]).then_inc(x_in[t], 16)
            sp.dma_start(kA[KR:KM, :, :], ones).then_inc(ones_in, 16)
            for n, (kind, i) in enumerate(halves):
                sp.wait_ge(part3, n + 1)
                for slot in range(len(Q_SLOTS)):
                    rows = slice(slot * D, (slot + 1) * D)
                    if kind == "k":
                        sp.dma_start(kA[rows, :, i * HALF:(i + 1) * HALF],
                                     parts[:, n % 3, K_SLOTS[slot], :]).then_inc(stacked[n], 16)
                    else:
                        c, hh = i
                        sp.dma_start(qA[rows, hh, 2 * c:2 * c + 2, :, :].rearrange("d a h n -> d (a h) n"),
                                     parts[:, n % 3, Q_SLOTS[slot], :]).then_inc(stacked[n], 16)

            def maxima_row(g, half, count):
                sp.dma_start(qA[KR:KM, half, bass.ds(g, 1), :, :].rearrange("p a h (r c) -> p (a h r) c", c=P),
                             maxT[:, half, :]).then_inc(max_in, 16)

            sp.wait_ge(pj_act, emptied(PJ_AT["max0", 0])[1])
            maxima_row(0, 0, 0)

            def step(g, more):
                sp.wait_ge(st_free, st_max1(g) + 1)
                sp.wait_ge(max_in, 16 * (2 * g + 1))
                maxima_row(g, 1, 2 * g + 1)
                if more:
                    sp.wait_ge(st_free, st_max0(g) + 1)
                    sp.wait_ge(max_in, 16 * (2 * g + 2))
                    maxima_row(g + 1, 0, 2 * g + 2)

            step(0, True)
            with sp.Fori(1, LAST) as g:
                step(g, True)
            step(LAST, False)
            cols = (KV - 2) * REP * D
            o_t = out.rearrange("(t p) n -> p t n", p=P)
            sp.wait_ge(group_done, 2 * (KV - 2))
            sp.dma_start(o_t[:, :, 0:cols], x_sb[:, :, 0:cols]).then_inc(stored, 16)
            for half in range(2):
                sp.wait_ge(group_done, 2 * LAST + half + 1)
                ts = slice(half * TH, (half + 1) * TH)
                sp.dma_start(o_t[:, ts, cols:E], x_sb[:, ts, cols:E]).then_inc(stored, 16)
            sp.wait_ge(stored, 48)

        @block.gpsimd
        def _(pool):
            for n, v in enumerate((-0.5, 0.5, -1.0, 0.0)):
                pool.memset(consts[:, n:n + 1], v).then_inc(const_set, 1)
            pool.memset(vg[:, :, D + 1:VC], 0.0).then_inc(const_set, 1)
            pool.memset(vg[:, :, D:D + 1], 1.0).then_inc(const_set, 1)
            pool.wait_ge(const_set, 6)
            for t in range(NT):
                pool.wait_ge(mean_var, t + 1)
                pool.tensor_scalar(mv[:, t, 1:2], mv[:, t, 1:2], EPS_LN, None, ALU.add).then_inc(eps_added, 1)
                pool.wait_ge(eps_added, t + 1)
                pool.tensor_tensor(rstd[:, t:t + 1], mv[:, t, 1:2], consts[:, 0:1], ALU.pow).then_inc(rstd_done, 1)

            def split(n):
                b2 = n % 2
                pool.wait_ge(sin_mul, n + 1)
                pool.tensor_tensor(rot[:, b2, :], rot[:, b2, :], swp[:, b2, :], ALU.add).then_inc(rotated, 1)
                pool.wait_ge(part1, n + 1)
                pool.tensor_tensor(rot[:, b2, :], rot[:, b2, :], parts[:, n % 3, 0, :],
                                   ALU.subtract).then_inc(left1, 1)
                pool.wait_ge(part2, n + 1)
                pool.tensor_tensor(parts[:, n % 3, 2, :], rot[:, b2, :], parts[:, n % 3, 1, :],
                                   ALU.subtract).then_inc(part3, 1)

            for n in range(len(halves)):
                split(n)

            def gamma(t):
                pool.wait_ge(norm_done, 2 * t + 2)
                pool.tensor_tensor(gam[:, t, :], norms[:, t, :], consts[:, 1:2].broadcast_to((P, 2)),
                                   ALU.pow).then_inc(pow_step, 1)
                pool.wait_ge(pow_step, 4 * t + 1)
                pool.tensor_scalar(gam[:, t, 1:2], gam[:, t, 1:2], EPS_M, None, ALU.add).then_inc(pow_step, 1)
                pool.wait_ge(pow_step, 4 * t + 2)
                pool.tensor_tensor(gam[:, t, 1:2], gam[:, t, 1:2], consts[:, 2:3], ALU.pow).then_inc(pow_step, 1)
                pool.wait_ge(pow_step, 4 * t + 3)
                pool.tensor_tensor(gam[:, t, 0:1], gam[:, t, 0:1], gam[:, t, 1:2], ALU.mult).then_inc(pow_step, 1)
                pool.wait_ge(pow_step, 4 * t + 4)
                pool.tensor_scalar(gam[:, t, 0:1], gam[:, t, 0:1], C_CLAMP, 1.0, ALU.mult,
                                   ALU.min).then_inc(gamma_done, 1)

            def gate(t):
                pool.wait_ge(gate_sig, t + 1)
                pool.tensor_tensor(z_sb[:, t, :], z_sb[:, t, :], m_sb[:, t % 3, :], ALU.mult).then_inc(gate_done, 1)

            def maxima(half, count, filled, emptied_by):
                pool.wait_ge(sm_free, filled)
                if emptied_by is not None:
                    pool.wait_ge(*emptied_by)
                pool.tensor_tensor(maxp[:, half, 0:16], negmax[:, half, :], consts[:, 3:4].broadcast_to((P, 16)),
                                   ALU.add).then_inc(max_hi, 1)
                pool.wait_ge(max_hi, count)
                pool.tensor_tensor(maxp[:, half, 16:32], negmax[:, half, :], maxp[:, half, 0:16],
                                   ALU.subtract).then_inc(max_parts, 1)

            def group_values(g):
                cols = bass.ds(g * D, D)
                pool.tensor_tensor(vg[:, :, 0:D], v_sb[:, :, cols],
                                   bv_sb[:, cols].unsqueeze(1).broadcast_to((P, NT, D)), ALU.add).then_inc(v_ready, 1)

            for t in range(NT):
                if t >= 3:
                    gate(t - 3)
                gamma(t)
                if t == 4:
                    maxima(0, 1, 16, None)
            pool.wait_ge(pj_dve, emptied(PJ_AT["v", 1])[1])
            pool.wait_ge(wv_in, 32)
            group_values(0)
            maxima(1, 2, 32, None)
            for t in range(NT - 3, NT):
                gate(t)

            def finish(g, half, n):
                pool.wait_ge(heads_scaled, n + 1)
                cols = bass.ds(g * (REP * D), REP * D)
                ts = slice(half * TH, (half + 1) * TH)
                pool.tensor_tensor(gated, scaled[:, :, :], z_sb[:, ts, cols], ALU.mult).then_inc(heads_gated, 1)
                pool.wait_ge(heads_gated, n + 1)
                pool.tensor_tensor(x_sb[:, ts, cols], x_sb[:, ts, cols], gated, ALU.add).then_inc(group_done, 1)

            def step(g, first=False, last=False):
                if not first:
                    pool.wait_ge(pv_done, 16 * g)
                    group_values(g)
                    finish(g - 1, 1, 2 * g - 1)
                if not last:
                    maxima(0, 2 * g + 3, sm_score(g, 15) + 1,
                           (pj_full, PJ_AT["max0", 0] + 1) if first else (st_full, st_max0(g - 1) + 1))
                finish(g, 0, 2 * g)
                if not last:
                    maxima(1, 2 * g + 4, sm_score(g, 31) + 1, (st_full, st_max1(g) + 1))

            step(0, first=True)
            with pool.Fori(1, LAST) as g:
                step(g)
            step(LAST, last=True)
            finish(LAST, 1, 2 * LAST + 1)

        @block.scalar
        def _(act):
            act.dma_start(id_sb[:, :], ident).then_inc(small_in, 16)
            act.dma_start(idb_sb[:, :], identb).then_inc(small_in, 16)
            act.dma_start(wk_sb[:, :, :], wk.rearrange("(c p) n -> p c n", p=P)).then_inc(wk_in, 16)
            wq_v = wq.rearrange("(c p) n -> p c n", p=P)
            act.dma_start(bias[:, :, :], biases).then_inc(small_in, 16)
            act.dma_start(cos_sb, cosT).then_inc(tab_in, 16)
            act.dma_start(sin_sb, sinT).then_inc(tab_in, 16)
            act.dma_start(wq_sb[:, :, 0:P], wq_v[:, :, 0:P]).then_inc(wq0_in, 16)
            act.dma_start(bv_sb[:, :], bv.partition_broadcast(P)).then_inc(wv_in, 16)
            act.dma_start(wv_sb[:, :, :], wv.rearrange("(c p) n -> p c n", p=P)).then_inc(wv_in, 16)
            act.dma_start(wq_sb[:, :, P:E], wq_v[:, :, P:E]).then_inc(wq_in, 16)
            act.dma_start(A_sb[:, :, :], A.rearrange("(c p) n -> p c n", p=P)).then_inc(ffn_in, 16)
            act.dma_start(p_sb[:, :], p_sc).then_inc(ffn_in, 16)
            act.dma_start(wT_sb[:, :, :], wT.rearrange("(c p) n -> p c n", p=P)).then_inc(ffn_in, 16)
            act.dma_start(B_sb[:, :], B).then_inc(ffn_in, 16)
            act.dma_start(b_sb[:, :], b.partition_broadcast(P)).then_inc(ffn_in, 16)

            for t in range(NT):
                act.wait_ge(pj_full, PJ_AT["xT", t] + 1)
                act.activation(xT[:, :, t * P:(t + 1) * P],
                               pj(PJ_AT["xT", t]).rearrange("p (c n) -> p c n", c=NE), ACT.Copy).then_inc(pj_act, 1)

            def cast(n):
                act.wait_ge(rotated, n + 1)
                if n >= 3:
                    act.wait_ge(stacked[n - 3], 16 * len(Q_SLOTS))
                act.activation(parts[:, n % 3, 0, :], rot[:, n % 2, :], ACT.Copy).then_inc(part1, 1)
                act.wait_ge(left1, n + 1)
                act.activation(parts[:, n % 3, 1, :], rot[:, n % 2, :], ACT.Copy).then_inc(part2, 1)

            for n in range(len(halves)):
                cast(n)

            act.wait_ge(ffn_in, 80)
            for hh in range(2):
                n = PJ_AT["u", hh]
                act.wait_ge(pj_full, n + 1)
                act.activation(uT[:, hh * HALF:(hh + 1) * HALF], pj(n), ACT.Copy,
                               scale=p_sb[:, 0:1]).then_inc(pj_act, 1)

            def gate_exp_of(t):
                act.wait_ge(gate_in, t + 1)
                act.activation(m_sb[:, t % 3, :], z_sb[:, t, :], ACT.Exp, scale=-1.0).then_inc(gate_exp, 1)

            for t in range(NT):
                n = PJ_AT["m", t]
                act.wait_ge(pj_full, n + 1)
                if t >= 3:
                    act.wait_ge(gate_done, t - 2)
                if t >= 1:
                    act.wait_ge(norm_done, 2 * t)
                act.activation(junk[:, 1, :], pj(n), ACT.Square,
                               accum_out=norms[:, t, 1:2]).then_inc(norm_done, 1)
                act.activation(m_sb[:, t % 3, :], pj(n), ACT.Copy).then_inc(pj_act, 1)
                act.wait_ge(pj_dve, emptied(PJ_AT["z", t])[1])
                act.activation(junk[:, 0, :], z_sb[:, t, :], ACT.Square,
                               accum_out=norms[:, t, 0:1]).then_inc(norm_done, 1)
                if t >= 2:
                    gate_exp_of(t - 2)
                if t == 5:
                    act.wait_ge(pj_full, PJ_AT["max0", 0] + 1)
                    act.activation(maxT[:, 0, :], pj(PJ_AT["max0", 0]).bitcast(BF16)[0:32, 0:P],
                                   ACT.Copy).then_inc(pj_act, 1)
            for t in range(NT - 2, NT):
                gate_exp_of(t)

            def evacuate(g, half, n, free):
                act.wait_ge(pv_done, 16 * g + 8 * (half + 1))
                if free is not None:
                    act.wait_ge(sm_full, free)
                act.activation(heads[:, half, :], oT[:, :], ACT.Copy).then_inc(heads_out, 1)

            def step(g, first=False, last=False):
                for s in range(16):
                    if s == MAX1_SLOT:
                        act.wait_ge(st_full, st_max1(g) + 1)
                        if not first:
                            act.wait_ge(max_in, 16 * 2 * g)
                        act.activation(maxT[:, 1, :], st[:, st_max1(0) % 3, :].bitcast(BF16)[0:32, 0:P],
                                       ACT.Copy).then_inc(st_free, 1)
                    if s == MAX0_SLOT and last:
                        pass
                    elif s == MAX0_SLOT:
                        act.wait_ge(st_full, st_max0(g) + 1)
                        act.wait_ge(max_in, 16 * (2 * g + 1))
                        act.activation(maxT[:, 0, :], st[:, st_max0(0) % 3, :].bitcast(BF16)[0:32, 0:P],
                                       ACT.Copy).then_inc(st_free, 1)
                    for h in range(REP):
                        late = 1 if last and s >= MAX0_SLOT else 0
                        act.wait_ge(st_full, st_score(g, s, h) + 1 - late)
                        if h == 0 and not (first and s < PB):
                            act.wait_ge(pv_done, 16 * g + s - PB + 1)
                        act.activation(probs[:, s % PB, h, :], st[:, (st_score(0, s, h) - late) % 3, :], ACT.Exp,
                                       scale=float(D) ** -0.5).then_inc(st_free, 1)
                        if s == 0 and h == 2 and not first:
                            evacuate(g - 1, 1, 2 * g - 1, sm_base(g - 1) + 2 * OUT1_SLOT + 1)
                        if s == 8 and h == 2:
                            evacuate(g, 0, 2 * g, None if first else sm_out0(g - 1) + 1)

            act.wait_ge(part3, len(halves))
            step(0, first=True)
            with act.Fori(1, LAST) as g:
                step(g)
            step(LAST, last=True)
            evacuate(LAST, 1, 2 * LAST + 1, SM_LAST_OUT1 + 1)

        @block.vector
        def _(dve):
            def normalise(t):
                dve.wait_ge(rstd_done, t + 1)
                if t >= 2:
                    dve.wait_ge(pj_full, PJ_AT["xT", t - 2] + 1)
                dve.tensor_scalar(xn[:, t % 2, :], x_sb[:, t, :], mv[:, t, 0:1], rstd[:, t:t + 1],
                                  ALU.subtract, ALU.mult).then_inc(xn_done, 1)

            for t in range(NT):
                dve.wait_ge(x_in[t], 16)
                dve.bn_stats(stats[:, t, :], x_sb[:, t, :]).then_inc(stats_done, 1)
                dve.wait_ge(stats_done, t + 1)
                dve.bn_aggr(mv[:, t, :], stats[:, t, :]).then_inc(mean_var, 1)
                if t >= 1:
                    normalise(t - 1)
            normalise(NT - 1)

            def rope(kind, i):
                n = halves.index((kind, i))
                col = CHUNKS if kind == "k" else i[0]
                hh = i if kind == "k" else i[1]
                e = PJ_AT[kind, i]
                tok = slice(hh * HALF, (hh + 1) * HALF)
                dve.wait_ge(pj_full, e + 1)
                if n >= 2:
                    dve.wait_ge(part3, n - 1)
                dve.scalar_tensor_tensor(rot[:, n % 2, :], pj(e), bias[:, col, 0:1], cos_sb[:, tok],
                                         ALU.add, ALU.mult).then_inc(cos_mul, 1)
                dve.stream_shuffle(swp[:, n % 2, :], pj(e), PARTNER).then_inc(pj_dve, 1)
                dve.wait_ge(pj_dve, emptied(e)[1])
                dve.scalar_tensor_tensor(swp[:, n % 2, :], swp[:, n % 2, :], bias[:, col, 1:2], sin_sb[:, tok],
                                         ALU.add, ALU.mult).then_inc(sin_mul, 1)

            dve.wait_ge(small_in, 48)
            dve.wait_ge(tab_in, 32)
            for hh in range(2):
                rope("k", hh)
            for hh in range(2):
                rope("q", (0, hh))
            for hh in range(2):
                e = PJ_AT["v", hh]
                dve.wait_ge(pj_full, e + 1)
                dve.tensor_copy(v_sb[:, hh * TH:(hh + 1) * TH, :],
                                pj(e).rearrange("p (t n) -> p t n", t=TH)).then_inc(pj_dve, 1)
            for c in range(1, CHUNKS):
                for hh in range(2):
                    rope("q", (c, hh))
            dve.wait_ge(ffn_in, 80)

            def row_max(n_full, bank, half, r, parts_done):
                dve.wait_ge(sm_full, n_full)
                if parts_done is not None:
                    dve.wait_ge(max_parts, parts_done)
                dve.tensor_reduce(negmax[:, half, r:r + 1], sm[:, bank, :], AX.X, ALU.max,
                                  negate=True).then_inc(sm_free, 1)

            def gate_sum(t):
                dve.wait_ge(gamma_done, t + 1)
                dve.wait_ge(pj_act, emptied(PJ_AT["m", t])[1])
                dve.scalar_tensor_tensor(z_sb[:, t, :], m_sb[:, t % 3, :], gam[:, t, 0:1], z_sb[:, t, :],
                                         ALU.mult, ALU.add).then_inc(gate_in, 1)

            def gate_sigmoid(t):
                dve.wait_ge(gate_exp, t + 1)
                dve.tensor_scalar(m_sb[:, t % 3, :], m_sb[:, t % 3, :], 1.0, None, ALU.add).then_inc(exp_plus1, 1)
                dve.wait_ge(exp_plus1, t + 1)
                dve.reciprocal(m_sb[:, t % 3, :], m_sb[:, t % 3, :]).then_inc(gate_sig, 1)

            for t in range(NT):
                e = PJ_AT["z", t]
                dve.wait_ge(pj_full, e + 1)
                dve.tensor_tensor(z_sb[:, t, :], pj(e), b_sb[:, :], ALU.add).then_inc(pj_dve, 1)
                for n in range(4 * t, 4 * t + 4):
                    row_max(n + 1, n % 2, n // 16, n % 16, None)
                    if n % 4 == 0 and t >= 3:
                        gate_sigmoid(t - 3)
                    if n % 4 == 2 and t >= 1:
                        gate_sum(t - 1)

            def scale_heads(n_full, bank, n):
                turned = sm[:, bank, 0:HALF].rearrange("p (t h c) -> p t h c", t=TH, h=REP)
                dve.wait_ge(sm_full, n_full)
                if n is not None:
                    dve.wait_ge(group_done, n)
                n = 0 if n is None else n
                dve.reciprocal(rsum[:, :].rearrange("p (t h) -> p t h", t=TH), turned[:, :, :, D]).then_inc(sums_inv, 1)
                dve.wait_ge(sums_inv, n + 1)
                dve.tensor_tensor(scaled[:, :, :].rearrange("p t (h d) -> p t h d", h=REP), turned[:, :, :, 0:D],
                                  rsum[:, :].rearrange("p (t h) -> p t h", t=TH).unsqueeze(3)
                                  .broadcast_to((P, TH, REP, D)), ALU.mult).then_inc(heads_scaled, 1)
                dve.wait_ge(heads_scaled, n + 1)
                dve.sem_inc(sm_free, 1)

            def step(g, first=False):
                for e in range(32):
                    if e == 2 * OUT1_SLOT and not first:
                        scale_heads(sm_out1(g) + 1, sm_out1(0) % 2, 2 * g - 1)
                    if e == 2 * OUT0_SLOT:
                        scale_heads(sm_out0(g) + 1, sm_out0(0) % 2, None if first else 2 * g)
                    row_max(sm_score(g, e, first) + 1, sm_score(0, e, first) % 2, e // 16, e % 16,
                            2 * g + e // 16 + 1 if e % 16 == 0 else None)
                    if first and e == 1:
                        gate_sum(NT - 1)
                    if first and e in (3, 5, 8):
                        gate_sigmoid({3: NT - 3, 5: NT - 2, 8: NT - 1}[e])

            step(0, first=True)
            with dve.Fori(1, LAST) as g:
                step(g)
            scale_heads(SM_LAST_OUT1 + 1, SM_LAST_OUT1 % 2, 2 * LAST - 1)
            scale_heads(SM_LAST_OUT0 + 1, SM_LAST_OUT0 % 2, 2 * LAST)
            scale_heads(SM_TAIL_OUT1 + 1, SM_TAIL_OUT1 % 2, 2 * LAST + 1)

        @block.tensor
        def _(pe):
            def claim(n):
                if n >= 4:
                    who, count = emptied(n - 4)
                    pe.wait_ge(pj_act if who == "act" else pj_dve, count)

            def project(kind, i, weight, columns, moving_tokens):
                n = PJ_AT[kind, i]
                claim(n)
                for c in range(NE):
                    mm = pe.matmul(pj(n), weight[:, c, columns], xT[:, c, moving_tokens],
                                   start=(c == 0), stop=(c == NE - 1))
                mm.then_inc(pj_full, 1)

            def half_tokens(hh):
                return slice(hh * HALF, (hh + 1) * HALF)

            pe.wait_ge(small_in, 48)
            for t in range(NT):
                n = PJ_AT["xT", t]
                pe.wait_ge(xn_done, t + 1)
                claim(n)
                for c in range(NE):
                    mm = pe.transpose(pj(n)[:, c * P:(c + 1) * P], xn[:, t % 2, c * P:(c + 1) * P], id_sb[:, :])
                mm.then_inc(pj_full, 1)
            pe.wait_ge(wk_in, 16)
            for hh in range(2):
                pe.wait_ge(pj_act, TH * (hh + 1))
                project("k", hh, wk_sb, slice(0, P), half_tokens(hh))
            pe.wait_ge(wq0_in, 16)
            for hh in range(2):
                project("q", (0, hh), wq_sb, slice(0, P), half_tokens(hh))
            pe.wait_ge(wv_in, 32)
            for hh in range(2):
                n = PJ_AT["v", hh]
                claim(n)
                for t in range(TH):
                    tok = slice((hh * TH + t) * P, (hh * TH + t + 1) * P)
                    for c in range(NE):
                        mm = pe.matmul(pj(n)[:, t * P:(t + 1) * P], xT[:, c, tok], wv_sb[:, c, :],
                                       start=(c == 0), stop=(c == NE - 1))
                mm.then_inc(pj_full, 1)
            pe.wait_ge(wq_in, 16)
            for c in range(1, CHUNKS):
                for hh in range(2):
                    project("q", (c, hh), wq_sb, slice(c * P, (c + 1) * P), half_tokens(hh))
            pe.wait_ge(ffn_in, 80)
            for hh in range(2):
                project("u", hh, A_sb, slice(0, RANK), half_tokens(hh))

            def score_rows(g, e, n, bank, freed):
                half, h, qt = e // 16, (e % 16) // TH, e % TH
                if freed is not None:
                    pe.wait_ge(sm_free, freed)
                for kh in range(2):
                    mm = pe.matmul(sm[:, bank, kh * HALF:(kh + 1) * HALF],
                                   qA[0:KR, half, bass.ds(g, 1), h, qt * P:(qt + 1) * P]
                                   .rearrange("p a n -> p (a n)"),
                                   kA[0:KR, bass.ds(g, 1), kh * HALF:(kh + 1) * HALF].rearrange("p a n -> p (a n)"),
                                   start=True, stop=True)
                mm.then_inc(sm_full, 1)

            def turn_maxima(out_bank, half):
                return pe.transpose(out_bank.bitcast(BF16)[0:32, 0:P], maxp[:, half, :], idb_sb[:, :])

            for n in range(4):
                pe.wait_ge(stacked[n], 16 * len(Q_SLOTS))
            pe.wait_ge(const_set, 6)
            pe.wait_ge(ones_in, 16)
            for t in range(NT):
                tok = slice(t * P, (t + 1) * P)
                n = PJ_AT["z", t]
                claim(n)
                for c in range(NE):
                    mm = pe.matmul(pj(n), xT[:, c, tok], wT_sb[:, c, :], start=(c == 0), stop=(c == NE - 1))
                mm.then_inc(pj_full, 1)
                for e in range(4 * t, 4 * t + 4):
                    score_rows(0, e, e, e % 2, e - 1 if e >= 2 else None)
                n = PJ_AT["m", t]
                claim(n)
                pe.wait_ge(pj_act, emptied(PJ_AT["u", t // TH])[1])
                pe.matmul(pj(n), uT[:, tok], B_sb[:, :], start=True, stop=True).then_inc(pj_full, 1)
                if t == 5:
                    n = PJ_AT["max0", 0]
                    claim(n)
                    pe.wait_ge(max_parts, 1)
                    turn_maxima(pj(n), 0).then_inc(pj_full, 1)
            pe.wait_ge(pj_act, sum(w == "act" for _, _, w in PJ))
            pe.wait_ge(pj_dve, sum(w == "dve" for _, _, w in PJ))
            for n in range(4, len(halves)):
                pe.wait_ge(stacked[n], 16 * len(Q_SLOTS))

            def values(g, s, exps, free):
                kt = s % NT
                pe.wait_ge(st_free, exps)
                if kt == 0:
                    if free is not None:
                        pe.wait_ge(heads_out, free)
                    if s == 0:
                        pe.wait_ge(v_ready, g + 1)
                for h in range(REP):
                    mm = pe.matmul(oT[h * VC:(h + 1) * VC, :], vg[:, kt, :], probs[:, s % PB, h, :],
                                   start=(kt == 0), stop=(kt == NT - 1))
                mm.then_inc(pv_done, 1)

            def turn_heads(half, bank, n_heads, freed):
                pe.wait_ge(heads_out, n_heads)
                pe.wait_ge(sm_free, freed)
                for t in range(TH):
                    mm = pe.transpose(sm[:, bank, t * P:(t + 1) * P], heads[:, half, t * P:(t + 1) * P], id_sb[:, :])
                mm.then_inc(sm_full, 1)

            def step(g, first=False, last=False):
                for s in range(16):
                    half, kt = s // NT, s % NT
                    late = 1 if last and s >= MAX0_SLOT else 0

                    def score_cols(h):
                        n = st_score(g, s, h) - late
                        if not (first and s == 0 and h < 3):
                            pe.wait_ge(st_free, n - 2)
                        pe.matmul(st[:, (st_score(0, s, h) - late) % 3, :],
                                  kA[:, bass.ds(g, 1), kt * P:(kt + 1) * P].rearrange("p a n -> p (a n)"),
                                  qA[:, half, bass.ds(g, 1), h, :].rearrange("p a n -> p (a n)"),
                                  start=True, stop=True).then_inc(st_full, 1)

                    def next_rows(e):
                        if not last:
                            n = sm_score(g, e, first)
                            score_rows(g + 1, e, n, sm_score(0, e, first) % 2, n - 1)

                    if s == MAX1_SLOT:
                        pe.wait_ge(max_parts, 2 * g + 2)
                        pe.wait_ge(st_free, st_max1(g) - 2)
                        turn_maxima(st[:, st_max1(0) % 3, :], 1).then_inc(st_full, 1)
                    if s == MAX0_SLOT and not last:
                        pe.wait_ge(max_parts, 2 * g + 3)
                        pe.wait_ge(st_free, st_max0(g) - 2)
                        turn_maxima(st[:, st_max0(0) % 3, :], 0).then_inc(st_full, 1)
                    if s % NT == 0:
                        pe.wait_ge(max_in, 16 * (2 * g + half + 1))
                    score_cols(0)
                    if s == OUT1_SLOT and not first:
                        n = SM_LAST_OUT1 if last else sm_out1(g)
                        turn_heads(1, (SM_LAST_OUT1 if last else sm_out1(0)) % 2, 2 * g, n - 1)
                    if s == OUT0_SLOT:
                        n = SM_LAST_OUT0 if last else sm_out0(g)
                        turn_heads(0, (SM_LAST_OUT0 if last else sm_out0(0)) % 2, 2 * g + 1, n - 1)
                    next_rows(2 * s)
                    score_cols(1)
                    if s > 0:
                        values(g, s - 1, st_score(g, s - 1, 3) + 1 - (1 if last and s - 1 >= MAX0_SLOT else 0),
                               None if first and s == 1 else 2 * g + half_of(s - 1))
                    elif not first:
                        values(g - 1, 15, st_score(g - 1, 15, 3) + 1, None)
                    score_cols(2)
                    next_rows(2 * s + 1)
                    score_cols(3)

            def half_of(s):
                return s // NT

            step(0, first=True)
            with pe.Fori(1, LAST) as g:
                step(g)
            step(LAST, last=True)
            values(LAST, 15, st_score(LAST, 15, 3), None)
            turn_heads(1, SM_TAIL_OUT1 % 2, 2 * LAST + 2, SM_TAIL_OUT1 - 1)


def kernel(L0_attn_x, L0_attn_wq, L0_attn_bq, L0_attn_wk, L0_attn_bk, L0_attn_wv, L0_attn_bv,
           L0_ffn_W, L0_ffn_b, L0_ffn_A, L0_ffn_B, L0_ffn_p_scores):
    import concourse.bacc as bacc
    from concourse.bass_utils import run_bass_kernel_spmd

    def rows(a):
        a = np.asarray(a)
        a = a.reshape(*a.shape[:-1], -1, KV, D)[..., ROW_ORDER]
        return np.moveaxis(a, -1, -2).reshape(*a.shape[:-3], -1)

    def columns(a):
        own = a.reshape(-1, D, KV)
        partner = own.reshape(-1, D // 2, 2, KV)[:, :, ::-1].reshape(own.shape)
        return np.stack([own, partner], -1).reshape(-1, P, 2)

    inv_freq = np.float32(1.0) / np.float32(10000.0) ** (np.arange(0, D, 2, dtype=np.float32) / np.float32(D))
    ang = np.arange(S, dtype=np.float32)[:, None] * inv_freq[None, :]
    sign = np.array([-1.0 if d < D // 2 else 1.0 for d in ROW_ORDER], np.float32)
    pair = [d % (D // 2) for d in ROW_ORDER]
    cosT = np.repeat(np.cos(ang).T[pair], KV, axis=0)
    sinT = np.repeat(np.sin(ang).T[pair] * sign[:, None], KV, axis=0)

    f = {
        "x": np.asarray(L0_attn_x).reshape(S, E),
        "wq": rows(L0_attn_wq),
        "wk": rows(L0_attn_wk),
        "wv": np.asarray(L0_attn_wv),
        "biases": np.concatenate([columns(rows(L0_attn_bq)), columns(rows(L0_attn_bk))]).transpose(1, 0, 2),
        "bv": np.asarray(L0_attn_bv),
        "wT": np.asarray(L0_ffn_W).T,
        "b": np.asarray(L0_ffn_b),
        "A": np.asarray(L0_ffn_A).transpose(1, 0, 2).reshape(E, RANK),
        "B": np.asarray(L0_ffn_B).reshape(RANK, E),
        "p_sc": np.repeat(np.asarray(L0_ffn_p_scores), RANK // len(L0_ffn_p_scores))[:, None],
        "cosT": cosT.astype(np.float32),
        "sinT": sinT.astype(np.float32),
        "ident": np.eye(P, dtype=np.float32),
        "ones": np.ones((KM - KR, KV, S), np.float32).astype(mybir.dt.np(BF16)),
        "identb": np.eye(P, dtype=np.float32).astype(mybir.dt.np(BF16)),
    }
    nc = bacc.Bacc("TRN2", target_bir_lowering=False, num_devices=1)
    arrays = {f"in_{k}": np.ascontiguousarray(v) for k, v in f.items()}
    args = {k: nc.dram_tensor(f"in_{k}", v.shape, mybir.dt.from_np(v.dtype), kind="ExternalInput").ap()
            for k, v in ((k, arrays[f"in_{k}"]) for k in f)}
    out = nc.dram_tensor("out", (S, E), F32, kind="ExternalOutput").ap()
    build(nc, out=out, **args)
    r = run_bass_kernel_spmd(nc, [arrays], core_ids=[0])
    return r.results[0]["out"].reshape(1, S, E)
```

```python
from contextlib import ExitStack

import numpy as np

import concourse.bass as bass
from concourse import mybir
from concourse.alu_op_type import AluOpType as ALU

F32 = mybir.dt.float32
BF16 = mybir.dt.bfloat16
ACT = mybir.ActivationFunctionType
AX = mybir.AxisListType

P = 128
S = 1024
E = 512
H, KV = 32, 8
D = E // H
REP = H // KV
NT = S // P
NE = E // P
HALF = S // 2
TH = NT // 2
CHUNKS = H // KV
RANK = 128
PARTS = 3
Q_SLOTS = (0, 1, 0, 1, 0, 2)
K_SLOTS = (0, 0, 1, 1, 2, 0)
KR = D * len(Q_SLOTS)
KM = KR + 2
VC = 32
PB = 4
ROW_ORDER = [j // 2 + (D // 2) * (j % 2) for j in range(D)]
PARTNER = [i ^ 8 for i in range(32)]
C_CLAMP, EPS_LN, EPS_M = 0.5, 1e-5, 1e-6

PJ = ([("xT", t, "act") for t in range(NT)]
      + [("k", hh, "dve") for hh in range(2)]
      + [("q", (0, hh), "dve") for hh in range(2)]
      + [("v", hh, "dve") for hh in range(2)]
      + [("q", (1, hh), "dve") for hh in range(2)])
MIXED = [("q", (2, 0), 3), ("q", (2, 1), 3), ("u", 0, 3), ("u", 1, 4), ("z", 0, 3), ("q", (3, 0), 3), ("z", 1, 3),
         ("q", (3, 1), 3), ("z", 2, 4), ("z", 3, 3)]
for _kind, _i, _rows in MIXED:
    PJ += [(_kind, _i, "act" if _kind == "u" else "dve")]
    if _kind == "z":
        PJ += [("m", _i, "act")]
    if (_kind, _i) == ("q", (3, 1)):
        PJ += [("max0", 0, "act")]
PJ_AT = {(kind, i): n for n, (kind, i, _) in enumerate(PJ)}


def emptied(n):
    who = PJ[n][2]
    return who, sum(w == who for _, _, w in PJ[:n + 1])


ST_PER, SM_PER = 66, 34
MAX1_SLOT, MAX0_SLOT = 2, 10
OUT1_SLOT, OUT0_SLOT = 2, 10


def st_score(g, s, h):
    return ST_PER * g + 4 * s + h + (s >= MAX1_SLOT) + (s >= MAX0_SLOT)


def st_max1(g):
    return ST_PER * g + 4 * MAX1_SLOT


def st_max0(g):
    return ST_PER * g + 4 * MAX0_SLOT + 1


def sm_base(g):
    return 31 + SM_PER * g


def sm_score(g, e, first=False):
    return sm_base(g) + e + (1 if e >= 2 * OUT1_SLOT else 0) + (1 if e >= 2 * OUT0_SLOT else 0) \
        + (1 if first and e < 2 * OUT1_SLOT else 0)


def sm_out1(g):
    return sm_base(g) + 2 * OUT1_SLOT


def sm_out0(g):
    return sm_base(g) + 2 * OUT0_SLOT + 1


LAST = KV - 1
SM_LAST = {what: sm_base(LAST) + i for i, what in enumerate((4, "out1", 5, 6, 7, "out0", "tail"))}
LATE_UNITS = {0: [(4, 0), (4, 1), (4, 2)], 1: [(4, 3), (4, NE)], 3: [(5, 0), (5, 1), (5, 2)], 4: [(5, 3), (5, NE)],
              5: [(6, 0), (6, 1)], 6: [(6, 2), (6, 3)], 7: [(6, NE)], 8: [(7, 0), (7, 1)], 9: [(7, 2), (7, 3), (7, NE)]}


def build(nc, x, wq, wk, wv, biases, bv, wT, b, A, B, p_sc, cosT, sinT, ident, identb, ones, out):
    ctx = ExitStack()
    with ctx:
        def sb(name, shape, dt=F32):
            return ctx.enter_context(nc.sbuf_tensor(name, shape, dt))

        def sem(name):
            return ctx.enter_context(nc.semaphore(name))

        x_sb = sb("x_sb", [P, NT, E])
        n_parts = 3 * PARTS * HALF // 2
        arena = sb("arena", [P, n_parts + 2 * HALF * 2 + NE * E + 2 * S])
        probs = arena[:, 0:PB * REP * HALF].rearrange("p (b h n) -> p b h n", b=PB, h=REP)

        def piece(start, *shape):
            letters = "abcd"[:len(shape)]
            return arena[:, start:start + int(np.prod(shape))].rearrange(
                f"p ({' '.join(letters)}) -> p {' '.join(letters)}", **dict(zip(letters, shape)))

        parts = arena[:, 0:n_parts].bitcast(BF16).rearrange("p (b k n) -> p b k n", b=3, k=PARTS)
        rot = piece(n_parts, 2, HALF)
        swp = piece(n_parts + 2 * HALF, 2, HALF)
        wq_sb = piece(n_parts + 4 * HALF, NE, E)
        tables = piece(n_parts + 4 * HALF + NE * E, 2, S)
        cos_sb, sin_sb = tables[:, 0, :], tables[:, 1, :]
        xT_sb = sb("xT_sb", [P, 2 * NE * HALF])
        xT = xT_sb[:, :].rearrange("p (h c n) -> p h c n", h=2, c=NE)
        late_gate = xT_sb[:, 0:NE * HALF].rearrange("p (t n) -> p t n", t=TH)
        wT_sb = sb("wT_sb", [P, NE, E])
        xn = sb("xn", [P, 2, E])
        wkv = sb("wkv", [P, 2, NE, P])
        wk_sb, wv_sb = wkv[:, 0, :, :], wkv[:, 1, :, :]
        heads = wkv[:, :, :, :].rearrange("p a c n -> p a (c n)")
        gated = sb("gated", [P, TH, REP * D])
        A_sb = sb("A_sb", [P, NE, RANK])
        B_sb = sb("B_sb", [RANK, E])
        uT = sb("uT", [RANK, S])
        qA = sb("qA", [KM, 2, KV, REP, HALF], BF16)
        kA = sb("kA", [KM, KV, S], BF16)
        z_sb = sb("z_sb", [P, TH, E])
        late_heads = sb("late_heads", [P, TH, E])
        m_sb = sb("m_sb", [P, 3, E])
        junk = sb("junk", [P, 2, E], BF16)
        v_sb = sb("v_sb", [P, NT, KV * D])
        vg = sb("vg", [P, NT, VC])
        id_sb = sb("id_sb", [P, P])
        idb_sb = sb("idb_sb", [P, P], BF16)
        b_sb = sb("b_sb", [P, E])
        bv_sb = sb("bv_sb", [P, KV * D])
        bias = sb("bias", [P, CHUNKS + 1, 2])
        p_sb = sb("p_sb", [RANK, 1])
        stats = sb("stats", [P, NT, 6])
        mv = sb("mv", [P, NT, 2])
        rstd = sb("rstd", [P, NT])
        consts = sb("consts", [P, 4])
        norms = sb("norms", [P, NT, 2])
        gam = sb("gam", [P, NT, 2])
        negmax = sb("negmax", [P, 2, 16])
        maxp = sb("maxp", [P, 2, 32], BF16)
        maxT = sb("maxT", [32, 2, P], BF16)
        rsum = sb("rsum", [P, TH * REP])
        scaled = sb("scaled", [P, TH, REP * D])

        sm = ctx.enter_context(nc.psum_tensor("sm", [P, 2, S], F32))
        st = ctx.enter_context(nc.psum_tensor("st", [P, 3, HALF], F32))
        oT = ctx.enter_context(nc.psum_tensor("oT", [P, HALF], F32))

        def pj(n):
            return oT[:, :] if n % 4 == 3 else st[:, n % 4, :]

        x_in = [sem(f"x_in{t}") for t in range(NT)]
        wk_in, wq0_in, wq_in, wv_in, tab_in, ffn_in, small_in = (sem(n) for n in (
            "wk_in", "wq0_in", "wq_in", "wv_in", "tab_in", "ffn_in", "small_in"))
        ones_in = sem("ones_in")
        const_set = sem("const_set")
        stats_done, mean_var, eps_added, rstd_done = (sem(n) for n in (
            "stats_done", "mean_var", "eps_added", "rstd_done"))
        xn_done = sem("xn_done")
        pj_full, pj_act, pj_dve = sem("pj_full"), sem("pj_act"), sem("pj_dve")
        cos_mul, swapped, sin_mul = sem("cos_mul"), sem("swapped"), sem("sin_mul")
        rotated, part1, left1, part2, part3 = (sem(n) for n in ("rotated", "part1", "left1", "part2", "part3"))
        stacked = [sem(f"stacked{n}") for n in range(2 + 2 * CHUNKS)]
        norm_done, pow_step, gamma_done = sem("norm_done"), sem("pow_step"), sem("gamma_done")
        gate_in, gate_exp, exp_plus1, gate_sig, gate_done = (sem(n) for n in (
            "gate_in", "gate_exp", "exp_plus1", "gate_sig", "gate_done"))
        sm_full, sm_free = sem("sm_full"), sem("sm_free")
        st_full, st_free = sem("st_full"), sem("st_free")
        max_hi, max_parts, max_in = sem("max_hi"), sem("max_parts"), sem("max_in")
        v_ready, pv_done = sem("v_ready"), sem("pv_done")
        heads_out, sums_inv, heads_scaled, heads_gated, group_done = (sem(n) for n in (
            "heads_out", "sums_inv", "heads_scaled", "heads_gated", "group_done"))
        late_copied, late_gated, late_scaled, late_added = (sem(n) for n in (
            "late_squared", "late_gated", "late_scaled", "late_added"))
        stored = sem("stored")

        halves = [("k", hh) for hh in range(2)] + [("q", (c, hh)) for c in range(CHUNKS) for hh in range(2)]

        def dense(t):
            return z_sb[:, t, :] if t < TH else late_gate[:, t - TH, :]

        LATE = (KV - 1) * REP * D

        block = ctx.enter_context(nc.Block())

        @block.sync
        def _(sp):
            for t in range(NT):
                sp.dma_start(x_sb[:, t, :], x[t * P:(t + 1) * P, :]).then_inc(x_in[t], 16)
            sp.dma_start(kA[KR:KM, :, :], ones).then_inc(ones_in, 16)
            for n, (kind, i) in enumerate(halves):
                sp.wait_ge(part3, n + 1)
                for slot in range(len(Q_SLOTS)):
                    rows = slice(slot * D, (slot + 1) * D)
                    if kind == "k":
                        sp.dma_start(kA[rows, :, i * HALF:(i + 1) * HALF],
                                     parts[:, n % 3, K_SLOTS[slot], :]).then_inc(stacked[n], 16)
                    else:
                        c, hh = i
                        sp.dma_start(qA[rows, hh, 2 * c:2 * c + 2, :, :].rearrange("d a h n -> d (a h) n"),
                                     parts[:, n % 3, Q_SLOTS[slot], :]).then_inc(stacked[n], 16)

            def maxima_row(g, half):
                sp.dma_start(qA[KR:KM, half, bass.ds(g, 1), :, :].rearrange("p a h (r c) -> p (a h r) c", c=P),
                             maxT[:, half, :]).then_inc(max_in, 16)

            sp.wait_ge(pj_act, emptied(PJ_AT["max0", 0])[1])
            maxima_row(0, 0)

            def step(g, more):
                sp.wait_ge(st_free, st_max1(g) + 1)
                sp.wait_ge(max_in, 16 * (2 * g + 1))
                maxima_row(g, 1)
                if more:
                    sp.wait_ge(st_free, st_max0(g) + 1)
                    sp.wait_ge(max_in, 16 * (2 * g + 2))
                    maxima_row(g + 1, 0)

            step(0, True)
            with sp.Fori(1, LAST) as g:
                step(g, True)
            step(LAST, False)
            o_t = out.rearrange("(t p) n -> p t n", p=P)
            sp.wait_ge(group_done, KV - 1)
            sp.dma_start(o_t[:, 0:TH, 0:LATE], x_sb[:, 0:TH, 0:LATE]).then_inc(stored, 16)
            for t in range(TH, NT):
                if t == NT - 1:
                    sp.wait_ge(group_done, KV)
                    sp.dma_start(o_t[:, 0:TH, LATE:E], x_sb[:, 0:TH, LATE:E]).then_inc(stored, 16)
                sp.wait_ge(late_added, t - TH + 1)
                sp.dma_start(o_t[:, t, 0:LATE], x_sb[:, t, 0:LATE]).then_inc(stored, 16)
            sp.wait_ge(group_done, KV + 1)
            sp.dma_start(o_t[:, TH:NT, LATE:E], x_sb[:, TH:NT, LATE:E]).then_inc(stored, 16)
            sp.wait_ge(stored, 16 * (TH + 3))

        @block.gpsimd
        def _(pool):
            for n, v in enumerate((-0.5, 0.5, -1.0, 0.0)):
                pool.memset(consts[:, n:n + 1], v).then_inc(const_set, 1)
            pool.memset(vg[:, :, D + 1:VC], 0.0).then_inc(const_set, 1)
            pool.memset(vg[:, :, D:D + 1], 1.0).then_inc(const_set, 1)
            pool.wait_ge(const_set, 6)
            for t in range(NT):
                pool.wait_ge(mean_var, t + 1)
                pool.tensor_scalar(mv[:, t, 1:2], mv[:, t, 1:2], EPS_LN, None, ALU.add).then_inc(eps_added, 1)
                pool.wait_ge(eps_added, t + 1)
                pool.tensor_tensor(rstd[:, t:t + 1], mv[:, t, 1:2], consts[:, 0:1], ALU.pow).then_inc(rstd_done, 1)

            def split(n):
                b2 = n % 2
                pool.wait_ge(sin_mul, n + 1)
                pool.tensor_tensor(rot[:, b2, :], rot[:, b2, :], swp[:, b2, :], ALU.add).then_inc(rotated, 1)
                pool.wait_ge(part1, n + 1)
                pool.tensor_tensor(rot[:, b2, :], rot[:, b2, :], parts[:, n % 3, 0, :],
                                   ALU.subtract).then_inc(left1, 1)
                pool.wait_ge(part2, n + 1)
                pool.tensor_tensor(parts[:, n % 3, 2, :], rot[:, b2, :], parts[:, n % 3, 1, :],
                                   ALU.subtract).then_inc(part3, 1)

            for n in range(len(halves) - 2):
                split(n)

            def gamma(t):
                pool.wait_ge(norm_done, 2 * t + 2)
                pool.tensor_tensor(gam[:, t, :], norms[:, t, :], consts[:, 1:2].broadcast_to((P, 2)),
                                   ALU.pow).then_inc(pow_step, 1)
                pool.wait_ge(pow_step, 4 * t + 1)
                pool.tensor_scalar(gam[:, t, 1:2], gam[:, t, 1:2], EPS_M, None, ALU.add).then_inc(pow_step, 1)
                pool.wait_ge(pow_step, 4 * t + 2)
                pool.tensor_tensor(gam[:, t, 1:2], gam[:, t, 1:2], consts[:, 2:3], ALU.pow).then_inc(pow_step, 1)
                pool.wait_ge(pow_step, 4 * t + 3)
                pool.tensor_tensor(gam[:, t, 0:1], gam[:, t, 0:1], gam[:, t, 1:2], ALU.mult).then_inc(pow_step, 1)
                pool.wait_ge(pow_step, 4 * t + 4)
                pool.tensor_scalar(gam[:, t, 0:1], gam[:, t, 0:1], C_CLAMP, 1.0, ALU.mult,
                                   ALU.min).then_inc(gamma_done, 1)

            def gate(t):
                pool.wait_ge(gate_sig, 4 * (t + 1))
                pool.tensor_tensor(z_sb[:, t, :], z_sb[:, t, :], m_sb[:, t % 3, :], ALU.mult).then_inc(gate_done, 1)

            def maxima(half, count, filled, emptied_by):
                pool.wait_ge(sm_free, filled)
                if emptied_by is not None:
                    pool.wait_ge(*emptied_by)
                pool.tensor_tensor(maxp[:, half, 0:16], negmax[:, half, :], consts[:, 3:4].broadcast_to((P, 16)),
                                   ALU.add).then_inc(max_hi, 1)
                pool.wait_ge(max_hi, count)
                pool.tensor_tensor(maxp[:, half, 16:32], negmax[:, half, :], maxp[:, half, 0:16],
                                   ALU.subtract).then_inc(max_parts, 1)

            def group_values(g):
                cols = bass.ds(g * D, D)
                pool.tensor_tensor(vg[:, :, 0:D], v_sb[:, :, cols],
                                   bv_sb[:, cols].unsqueeze(1).broadcast_to((P, NT, D)), ALU.add).then_inc(v_ready, 1)

            maxima(0, 1, 16, None)
            gamma(0)
            split(len(halves) - 2)
            gamma(1)
            split(len(halves) - 1)
            pool.wait_ge(pj_dve, emptied(PJ_AT["v", 1])[1])
            pool.wait_ge(wv_in, 32)
            group_values(0)
            gate(0)
            gamma(2)
            gate(1)
            gamma(3)
            maxima(1, 2, 32, None)

            def finish(g, half, n, gate_at):
                pool.wait_ge(heads_scaled, 2 * g + half + 1)
                cols = bass.ds(g * (REP * D), REP * D)
                ts = slice(half * TH, (half + 1) * TH)
                pool.tensor_tensor(gated[:, :, :], scaled[:, :, :], gate_at[:, :, cols],
                                   ALU.mult).then_inc(heads_gated, 1)
                pool.wait_ge(heads_gated, n + 1)
                pool.tensor_tensor(x_sb[:, ts, cols], x_sb[:, ts, cols], gated[:, :, :],
                                   ALU.add).then_inc(group_done, 1)

            def step(g, first=False):
                if not first:
                    pool.wait_ge(pv_done, 16 * g)
                    group_values(g)
                maxima(0, 2 * g + 3, sm_score(g, 15) + 1,
                       (pj_full, PJ_AT["max0", 0] + 1) if first else (st_full, st_max0(g - 1) + 1))
                finish(g, 0, g, z_sb)
                maxima(1, 2 * g + 4, sm_score(g, 31) + 1, (st_full, st_max1(g) + 1))

            gate(2)
            gate(3)
            step(0, first=True)
            with pool.Fori(1, LAST) as g:
                step(g)

            def add_late(t):
                pool.wait_ge(late_gated, t - TH + 1)
                held = late_heads[:, t - TH, 0:LATE]
                pool.tensor_tensor(held, held, late_gate[:, t - TH, 0:LATE], ALU.mult).then_inc(late_scaled, 1)
                pool.wait_ge(late_scaled, t - TH + 1)
                pool.tensor_tensor(x_sb[:, t, 0:LATE], x_sb[:, t, 0:LATE], held, ALU.add).then_inc(late_added, 1)

            pool.wait_ge(pv_done, 16 * LAST)
            group_values(LAST)
            gamma(4)
            gamma(5)
            add_late(4)
            gamma(6)
            add_late(5)
            gamma(7)
            add_late(6)
            finish(LAST, 0, LAST, z_sb)
            add_late(7)
            finish(LAST, 1, LAST + 1, late_gate)

        @block.scalar
        def _(act):
            act.dma_start(id_sb[:, :], ident).then_inc(small_in, 16)
            act.dma_start(idb_sb[:, :], identb).then_inc(small_in, 16)
            act.dma_start(wk_sb[:, :, :], wk.rearrange("(c p) n -> p c n", p=P)).then_inc(wk_in, 16)
            wq_v = wq.rearrange("(c p) n -> p c n", p=P)
            act.dma_start(bias[:, :, :], biases).then_inc(small_in, 16)
            act.dma_start(cos_sb, cosT).then_inc(tab_in, 16)
            act.dma_start(sin_sb, sinT).then_inc(tab_in, 16)
            act.dma_start(wq_sb[:, :, 0:P], wq_v[:, :, 0:P]).then_inc(wq0_in, 16)
            act.dma_start(bv_sb[:, :], bv.partition_broadcast(P)).then_inc(wv_in, 16)
            act.dma_start(wv_sb[:, :, :], wv.rearrange("(c p) n -> p c n", p=P)).then_inc(wv_in, 16)
            act.dma_start(wq_sb[:, :, P:E], wq_v[:, :, P:E]).then_inc(wq_in, 16)
            act.dma_start(A_sb[:, :, :], A.rearrange("(c p) n -> p c n", p=P)).then_inc(ffn_in, 16)
            act.dma_start(p_sb[:, :], p_sc).then_inc(ffn_in, 16)
            act.dma_start(wT_sb[:, :, :], wT.rearrange("(c p) n -> p c n", p=P)).then_inc(ffn_in, 16)
            act.dma_start(B_sb[:, :], B).then_inc(ffn_in, 16)
            act.dma_start(b_sb[:, :], b.partition_broadcast(P)).then_inc(ffn_in, 16)

            for t in range(NT):
                act.wait_ge(pj_full, PJ_AT["xT", t] + 1)
                act.activation(xT[:, t // TH, :, t % TH * P:(t % TH + 1) * P],
                               pj(PJ_AT["xT", t]).rearrange("p (c n) -> p c n", c=NE), ACT.Copy).then_inc(pj_act, 1)

            def cast(n):
                act.wait_ge(rotated, n + 1)
                if n >= 3:
                    act.wait_ge(stacked[n - 3], 16 * len(Q_SLOTS))
                act.activation(parts[:, n % 3, 0, :], rot[:, n % 2, :], ACT.Copy).then_inc(part1, 1)
                act.wait_ge(left1, n + 1)
                act.activation(parts[:, n % 3, 1, :], rot[:, n % 2, :], ACT.Copy).then_inc(part2, 1)

            for n in range(len(halves) - 2):
                cast(n)

            act.wait_ge(ffn_in, 80)
            for hh in range(2):
                n = PJ_AT["u", hh]
                act.wait_ge(pj_full, n + 1)
                act.activation(uT[:, hh * HALF:(hh + 1) * HALF], pj(n), ACT.Copy,
                               scale=p_sb[:, 0:1]).then_inc(pj_act, 1)

            def gate_exp_of(t):
                act.wait_ge(gate_in, t + 1)
                act.activation(m_sb[:, t % 3, :], dense(t), ACT.Exp, scale=-1.0).then_inc(gate_exp, 1)

            def squares(t):
                n = PJ_AT["m", t]
                act.wait_ge(pj_full, n + 1)
                if t >= 3:
                    act.wait_ge(gate_done, t - 2)
                if t >= 1:
                    act.wait_ge(norm_done, 2 * t)
                act.activation(junk[:, 1, :], pj(n), ACT.Square,
                               accum_out=norms[:, t, 1:2]).then_inc(norm_done, 1)
                act.activation(m_sb[:, t % 3, :], pj(n), ACT.Copy).then_inc(pj_act, 1)
                act.wait_ge(pj_dve, emptied(PJ_AT["z", t])[1])
                act.activation(junk[:, 0, :], z_sb[:, t, :], ACT.Square,
                               accum_out=norms[:, t, 0:1]).then_inc(norm_done, 1)

            squares(0)
            gate_exp_of(0)
            cast(len(halves) - 2)
            squares(1)
            gate_exp_of(1)
            cast(len(halves) - 1)
            act.wait_ge(pj_full, PJ_AT["max0", 0] + 1)
            act.activation(maxT[:, 0, :], pj(PJ_AT["max0", 0]).bitcast(BF16)[0:32, 0:P], ACT.Copy).then_inc(pj_act, 1)
            squares(2)
            gate_exp_of(2)
            squares(3)

            def evacuate(g, half, n, free):
                act.wait_ge(pv_done, 16 * g + 8 * (half + 1))
                if free is not None:
                    act.wait_ge(sm_full, free)
                act.activation(heads[:, half, :], oT[:, :], ACT.Copy).then_inc(heads_out, 1)

            def step(g, first=False, last=False):
                for s in range(16):
                    if s == MAX1_SLOT:
                        act.wait_ge(st_full, st_max1(g) + 1)
                        if not first:
                            act.wait_ge(max_in, 16 * 2 * g)
                        act.activation(maxT[:, 1, :], st[:, st_max1(0) % 3, :].bitcast(BF16)[0:32, 0:P],
                                       ACT.Copy).then_inc(st_free, 1)
                    if s == MAX0_SLOT and last:
                        pass
                    elif s == MAX0_SLOT:
                        act.wait_ge(st_full, st_max0(g) + 1)
                        act.wait_ge(max_in, 16 * (2 * g + 1))
                        act.activation(maxT[:, 0, :], st[:, st_max0(0) % 3, :].bitcast(BF16)[0:32, 0:P],
                                       ACT.Copy).then_inc(st_free, 1)
                    for h in range(REP):
                        late = 1 if last and s >= MAX0_SLOT else 0
                        act.wait_ge(st_full, st_score(g, s, h) + 1 - late)
                        if h == 0 and not (first and s < PB):
                            act.wait_ge(pv_done, 16 * g + s - PB + 1)
                        act.activation(probs[:, s % PB, h, :], st[:, (st_score(0, s, h) - late) % 3, :], ACT.Exp,
                                       scale=float(D) ** -0.5).then_inc(st_free, 1)
                        if first and (s, h) == (3, 3):
                            gate_exp_of(3)
                        if last and (s, h) in ((4, 3), (8, 3), (11, 3), (14, 3)):
                            gate_exp_of({4: 4, 8: 5, 11: 6, 14: 7}[s])
                        if s == 0 and h == 2 and not first:
                            evacuate(g - 1, 1, 2 * g - 1, sm_base(g - 1) + 2 * OUT1_SLOT + 1)
                        if s == 8 and h == 2:
                            evacuate(g, 0, 2 * g, None if first else sm_out0(g - 1) + 1)

            act.wait_ge(part3, len(halves))
            step(0, first=True)
            with act.Fori(1, LAST) as g:
                step(g)
            step(LAST, last=True)
            evacuate(LAST, 1, 2 * LAST + 1, SM_LAST["out1"] + 1)

        @block.vector
        def _(dve):
            def normalise(t):
                dve.wait_ge(rstd_done, t + 1)
                if t >= 2:
                    dve.wait_ge(pj_full, PJ_AT["xT", t - 2] + 1)
                dve.tensor_scalar(xn[:, t % 2, :], x_sb[:, t, :], mv[:, t, 0:1], rstd[:, t:t + 1],
                                  ALU.subtract, ALU.mult).then_inc(xn_done, 1)

            for t in range(NT):
                dve.wait_ge(x_in[t], 16)
                dve.bn_stats(stats[:, t, :], x_sb[:, t, :]).then_inc(stats_done, 1)
                dve.wait_ge(stats_done, t + 1)
                dve.bn_aggr(mv[:, t, :], stats[:, t, :]).then_inc(mean_var, 1)
                if t >= 1:
                    normalise(t - 1)
            normalise(NT - 1)

            def rope(kind, i):
                n = halves.index((kind, i))
                col = CHUNKS if kind == "k" else i[0]
                hh = i if kind == "k" else i[1]
                e = PJ_AT[kind, i]
                tok = slice(hh * HALF, (hh + 1) * HALF)
                dve.wait_ge(pj_full, e + 1)
                if n >= 2:
                    dve.wait_ge(part3, n - 1)
                dve.scalar_tensor_tensor(rot[:, n % 2, :], pj(e), bias[:, col, 0:1], cos_sb[:, tok],
                                         ALU.add, ALU.mult).then_inc(cos_mul, 1)
                dve.stream_shuffle(swp[:, n % 2, :], pj(e), PARTNER).then_inc(pj_dve, 1)
                dve.wait_ge(pj_dve, emptied(e)[1])
                dve.scalar_tensor_tensor(swp[:, n % 2, :], swp[:, n % 2, :], bias[:, col, 1:2], sin_sb[:, tok],
                                         ALU.add, ALU.mult).then_inc(sin_mul, 1)

            dve.wait_ge(small_in, 48)
            dve.wait_ge(tab_in, 32)
            for hh in range(2):
                rope("k", hh)
            for hh in range(2):
                rope("q", (0, hh))
            for hh in range(2):
                e = PJ_AT["v", hh]
                dve.wait_ge(pj_full, e + 1)
                dve.tensor_copy(v_sb[:, hh * TH:(hh + 1) * TH, :],
                                pj(e).rearrange("p (t n) -> p t n", t=TH)).then_inc(pj_dve, 1)
            for hh in range(2):
                rope("q", (1, hh))
            dve.wait_ge(ffn_in, 80)

            def row_max(n_full, bank, half, r, parts_done):
                dve.wait_ge(sm_full, n_full)
                if parts_done is not None:
                    dve.wait_ge(max_parts, parts_done)
                dve.tensor_reduce(negmax[:, half, r:r + 1], sm[:, bank, :], AX.X, ALU.max,
                                  negate=True).then_inc(sm_free, 1)

            def gate_sum(t):
                dve.wait_ge(gamma_done, t + 1)
                if t < TH:
                    dve.wait_ge(pj_act, emptied(PJ_AT["m", t])[1])
                dve.scalar_tensor_tensor(dense(t), m_sb[:, t % 3, :], gam[:, t, 0:1], dense(t),
                                         ALU.mult, ALU.add).then_inc(gate_in, 1)

            def gate_sigmoid(t, quarters=range(4)):
                for k in quarters:
                    if k == 0:
                        dve.wait_ge(gate_exp, t + 1)
                        dve.tensor_scalar(m_sb[:, t % 3, :], m_sb[:, t % 3, :], 1.0, None,
                                          ALU.add).then_inc(exp_plus1, 1)
                        dve.wait_ge(exp_plus1, t + 1)
                    q = slice(k * P, (k + 1) * P)
                    dve.reciprocal(m_sb[:, t % 3, q], m_sb[:, t % 3, q]).then_inc(gate_sig, 1)

            gate_work = {("q", (3, 0), 1): lambda: gate_sum(0),
                         ("z", 1, 0): lambda: gate_sigmoid(0, [0]), ("z", 1, 1): lambda: gate_sigmoid(0, [1]),
                         ("z", 1, 2): lambda: gate_sigmoid(0, [2]), ("q", (3, 1), 0): lambda: gate_sigmoid(0, [3]),
                         ("q", (3, 1), 1): lambda: gate_sum(1),
                         ("z", 2, 0): lambda: gate_sigmoid(1, [0]), ("z", 2, 1): lambda: gate_sigmoid(1, [1]),
                         ("z", 2, 2): lambda: gate_sigmoid(1, [2]), ("z", 2, 3): lambda: gate_sigmoid(1, [3]),
                         ("z", 3, 1): lambda: gate_sum(2)}
            n = 0
            for kind, i, rows in MIXED:
                for r in range(rows):
                    row_max(n + 1, n % 2, n // 16, n % 16, None)
                    n += 1
                    if (kind, i, r) in gate_work:
                        gate_work[kind, i, r]()
                if kind == "q":
                    rope("q", i)
                if kind == "z":
                    e = PJ_AT["z", i]
                    dve.wait_ge(pj_full, e + 1)
                    dve.tensor_tensor(z_sb[:, i, :], pj(e), b_sb[:, :], ALU.add).then_inc(pj_dve, 1)

            def scale_heads(n_full, bank, n, to, done):
                turned = sm[:, bank, 0:HALF].rearrange("p (t h c) -> p t h c", t=TH, h=REP)
                dve.wait_ge(sm_full, n_full)
                if done is not None:
                    dve.wait_ge(group_done, done)
                dve.reciprocal(rsum[:, :].rearrange("p (t h) -> p t h", t=TH), turned[:, :, :, D]).then_inc(sums_inv, 1)
                dve.wait_ge(sums_inv, n + 1)
                dve.tensor_tensor(to.rearrange("p t (h d) -> p t h d", h=REP), turned[:, :, :, 0:D],
                                  rsum[:, :].rearrange("p (t h) -> p t h", t=TH).unsqueeze(3)
                                  .broadcast_to((P, TH, REP, D)), ALU.mult).then_inc(heads_scaled, 1)
                dve.wait_ge(heads_scaled, n + 1)
                dve.sem_inc(sm_free, 1)

            def hold_heads(g, n_full, bank):
                scale_heads(n_full, bank, 2 * g + 1, late_heads[:, :, bass.ds(g * (REP * D), REP * D)], None)

            def step(g, first=False):
                for e in range(32):
                    if e == 2 * OUT1_SLOT and not first:
                        hold_heads(g - 1, sm_out1(g) + 1, sm_out1(0) % 2)
                    if e == 2 * OUT0_SLOT:
                        scale_heads(sm_out0(g) + 1, sm_out0(0) % 2, 2 * g, scaled[:, :, :], None if first else g)
                    row_max(sm_score(g, e, first) + 1, sm_score(0, e, first) % 2, e // 16, e % 16,
                            2 * g + e // 16 + 1 if e % 16 == 0 else None)
                    if first and e == 2:
                        gate_sum(3)
                    if first and 3 <= e < 7:
                        gate_sigmoid(2, [e - 3])
                    if first and 9 <= e < 13:
                        gate_sigmoid(3, [e - 9])

            step(0, first=True)
            with dve.Fori(1, LAST) as g:
                step(g)

            def late_dense(t):
                n = SM_LAST[t]
                unread = uT[:, 0:HALF]
                dve.wait_ge(sm_full, n + 1)
                dve.tensor_tensor(dense(t), sm[:, n % 2, 0:HALF], b_sb[:, :], ALU.add).then_inc(late_copied, 1)
                if t == TH:
                    dve.wait_ge(gate_done, TH)
                if t - 3 >= TH:
                    dve.wait_ge(late_gated, t - 3 - TH + 1)
                dve.tensor_copy(m_sb[:, t % 3, :], sm[:, n % 2, HALF:S]).then_inc(late_copied, 1)
                dve.wait_ge(late_copied, 2 * (t - TH) + 2)
                dve.sem_inc(sm_free, 1)
                for k, values in ((1, m_sb[:, t % 3, :]), (0, dense(t))):
                    dve.wait_ge(norm_done, 2 * t + 1 - k)
                    dve.scalar_tensor_tensor(unread, values, 1.0, values, ALU.mult, ALU.mult,
                                             accum_out=norms[:, t, k:k + 1]).then_inc(norm_done, 1)

            def late_silu(t):
                gate_sigmoid(t)
                dve.wait_ge(gate_sig, 4 * (t + 1))
                dve.tensor_tensor(dense(t), dense(t), m_sb[:, t % 3, :], ALU.mult).then_inc(late_gated, 1)

            late_dense(4)
            hold_heads(LAST - 1, SM_LAST["out1"] + 1, SM_LAST["out1"] % 2)
            gate_sum(4)
            late_dense(5)
            late_silu(4)
            gate_sum(5)
            late_dense(6)
            late_silu(5)
            gate_sum(6)
            late_dense(7)
            late_silu(6)
            gate_sum(7)
            scale_heads(SM_LAST["out0"] + 1, SM_LAST["out0"] % 2, 2 * LAST, scaled[:, :, :], LAST)
            late_silu(7)
            scale_heads(SM_LAST["tail"] + 1, SM_LAST["tail"] % 2, 2 * LAST + 1, scaled[:, :, :], LAST + 1)

        @block.tensor
        def _(pe):
            def claim(n):
                if n >= 4:
                    who, count = emptied(n - 4)
                    pe.wait_ge(pj_act if who == "act" else pj_dve, count)

            def project(kind, i, weight, columns, moving, rows=0):
                n = PJ_AT[kind, i]
                claim(n)
                for c in range(NE):
                    mm = pe.matmul(pj(n), weight[:, c, columns], moving[:, c, :], start=(c == 0), stop=(c == NE - 1))
                    if c == NE - 1:
                        mm.then_inc(pj_full, 1)
                    if c < rows:
                        next_maximum()

            pe.wait_ge(small_in, 48)
            for t in range(NT):
                n = PJ_AT["xT", t]
                pe.wait_ge(xn_done, t + 1)
                claim(n)
                for c in range(NE):
                    mm = pe.transpose(pj(n)[:, c * P:(c + 1) * P], xn[:, t % 2, c * P:(c + 1) * P], id_sb[:, :])
                mm.then_inc(pj_full, 1)
            pe.wait_ge(wk_in, 16)
            for hh in range(2):
                pe.wait_ge(pj_act, TH * (hh + 1))
                project("k", hh, wk_sb, slice(0, P), xT[:, hh])
            pe.wait_ge(wq0_in, 16)
            for hh in range(2):
                project("q", (0, hh), wq_sb, slice(0, P), xT[:, hh])
            pe.wait_ge(wv_in, 32)
            for hh in range(2):
                n = PJ_AT["v", hh]
                claim(n)
                for t in range(TH):
                    for c in range(NE):
                        mm = pe.matmul(pj(n)[:, t * P:(t + 1) * P], xT[:, hh, c, t * P:(t + 1) * P], wv_sb[:, c, :],
                                       start=(c == 0), stop=(c == NE - 1))
                mm.then_inc(pj_full, 1)
            pe.wait_ge(wq_in, 16)
            for hh in range(2):
                project("q", (1, hh), wq_sb, slice(P, 2 * P), xT[:, hh])

            def score_rows(g, e, n, bank, freed):
                half, h, qt = e // 16, (e % 16) // TH, e % TH
                if freed is not None:
                    pe.wait_ge(sm_free, freed)
                for kh in range(2):
                    mm = pe.matmul(sm[:, bank, kh * HALF:(kh + 1) * HALF],
                                   qA[0:KR, half, bass.ds(g, 1), h, qt * P:(qt + 1) * P]
                                   .rearrange("p a n -> p (a n)"),
                                   kA[0:KR, bass.ds(g, 1), kh * HALF:(kh + 1) * HALF].rearrange("p a n -> p (a n)"),
                                   start=True, stop=True)
                mm.then_inc(sm_full, 1)

            entries = iter(range(32))

            def next_maximum():
                e = next(entries)
                for n in {0: (0, 1, 2), 16: (3,)}.get(e, ()):
                    pe.wait_ge(stacked[n], 16 * len(Q_SLOTS))
                score_rows(0, e, e, e % 2, e - 1 if e >= 2 else None)

            def turn_maxima(out_bank, half):
                return pe.transpose(out_bank.bitcast(BF16)[0:32, 0:P], maxp[:, half, :], idb_sb[:, :])

            for kind, i, rows in MIXED:
                if kind == "q":
                    c, hh = i
                    project("q", i, wq_sb, slice(c * P, (c + 1) * P), xT[:, hh], rows)
                if (kind, i) == ("u", 0):
                    pe.wait_ge(ffn_in, 80)
                if kind == "u":
                    project("u", i, A_sb, slice(0, RANK), xT[:, i], rows)
                if kind == "z":
                    dense_tile = xT[:, i // TH, :, i % TH * P:(i % TH + 1) * P]
                    project("z", i, dense_tile, slice(0, P), wT_sb, rows)
                    n = PJ_AT["m", i]
                    claim(n)
                    pe.wait_ge(pj_act, emptied(PJ_AT["u", i // TH])[1])
                    pe.matmul(pj(n), uT[:, i * P:(i + 1) * P], B_sb[:, :], start=True, stop=True).then_inc(pj_full, 1)
                if (kind, i) == ("q", (3, 1)):
                    n = PJ_AT["max0", 0]
                    claim(n)
                    pe.wait_ge(max_parts, 1)
                    turn_maxima(pj(n), 0).then_inc(pj_full, 1)
            pe.wait_ge(const_set, 6)
            pe.wait_ge(ones_in, 16)
            pe.wait_ge(pj_act, sum(w == "act" for _, _, w in PJ))
            pe.wait_ge(pj_dve, sum(w == "dve" for _, _, w in PJ))
            for n in range(4, len(halves)):
                pe.wait_ge(stacked[n], 16 * len(Q_SLOTS))

            def values(g, s, exps, free):
                kt = s % NT
                pe.wait_ge(st_free, exps)
                if kt == 0:
                    if free is not None:
                        pe.wait_ge(heads_out, free)
                    if s == 0:
                        pe.wait_ge(v_ready, g + 1)
                for h in range(REP):
                    mm = pe.matmul(oT[h * VC:(h + 1) * VC, :], vg[:, kt, :], probs[:, s % PB, h, :],
                                   start=(kt == 0), stop=(kt == NT - 1))
                mm.then_inc(pv_done, 1)

            def turn_heads(half, bank, n_heads, freed):
                pe.wait_ge(heads_out, n_heads)
                pe.wait_ge(sm_free, freed)
                for t in range(TH):
                    mm = pe.transpose(sm[:, bank, t * P:(t + 1) * P], heads[:, half, t * P:(t + 1) * P], id_sb[:, :])
                mm.then_inc(sm_full, 1)

            def late_unit(t, c):
                n = SM_LAST[t]
                if c == 0:
                    pe.wait_ge(sm_free, n - 1)
                if c < NE:
                    pe.matmul(sm[:, n % 2, 0:HALF], xT[:, 1, c, (t - TH) * P:(t - TH + 1) * P], wT_sb[:, c, :],
                              start=(c == 0), stop=(c == NE - 1))
                else:
                    pe.matmul(sm[:, n % 2, HALF:S], uT[:, t * P:(t + 1) * P], B_sb[:, :],
                              start=True, stop=True).then_inc(sm_full, 1)

            def step(g, first=False, last=False):
                for s in range(16):
                    half, kt = s // NT, s % NT
                    fewer = 1 if last and s >= MAX0_SLOT else 0

                    def score_cols(h):
                        n = st_score(g, s, h) - fewer
                        if not (first and s == 0 and h < 3):
                            pe.wait_ge(st_free, n - 2)
                        pe.matmul(st[:, (st_score(0, s, h) - fewer) % 3, :],
                                  kA[:, bass.ds(g, 1), kt * P:(kt + 1) * P].rearrange("p a n -> p (a n)"),
                                  qA[:, half, bass.ds(g, 1), h, :].rearrange("p a n -> p (a n)"),
                                  start=True, stop=True).then_inc(st_full, 1)

                    def next_rows(e):
                        if not last:
                            n = sm_score(g, e, first)
                            score_rows(g + 1, e, n, sm_score(0, e, first) % 2, n - 1)

                    if s == MAX1_SLOT:
                        pe.wait_ge(max_parts, 2 * g + 2)
                        pe.wait_ge(st_free, st_max1(g) - 2)
                        turn_maxima(st[:, st_max1(0) % 3, :], 1).then_inc(st_full, 1)
                    if s == MAX0_SLOT and not last:
                        pe.wait_ge(max_parts, 2 * g + 3)
                        pe.wait_ge(st_free, st_max0(g) - 2)
                        turn_maxima(st[:, st_max0(0) % 3, :], 0).then_inc(st_full, 1)
                    if s % NT == 0:
                        pe.wait_ge(max_in, 16 * (2 * g + half + 1))
                    score_cols(0)
                    if s == OUT1_SLOT and not first:
                        n = SM_LAST["out1"] if last else sm_out1(g)
                        turn_heads(1, (n if last else sm_out1(0)) % 2, 2 * g, n - 1)
                    if s == OUT0_SLOT:
                        n = SM_LAST["out0"] if last else sm_out0(g)
                        turn_heads(0, (n if last else sm_out0(0)) % 2, 2 * g + 1, n - 1)
                    if last:
                        units = list(LATE_UNITS.get(s, ()))
                    next_rows(2 * s)
                    if last and units:
                        late_unit(*units.pop(0))
                    score_cols(1)
                    if s > 0:
                        values(g, s - 1, st_score(g, s - 1, 3) + 1 - (1 if last and s - 1 >= MAX0_SLOT else 0),
                               None if first and s == 1 else 2 * g + (s - 1) // NT)
                    elif not first:
                        values(g - 1, 15, st_score(g - 1, 15, 3) + 1, None)
                    if last and units:
                        late_unit(*units.pop(0))
                    score_cols(2)
                    next_rows(2 * s + 1)
                    if last and units:
                        late_unit(*units.pop(0))
                    score_cols(3)

            step(0, first=True)
            with pe.Fori(1, LAST) as g:
                step(g)
            step(LAST, last=True)
            values(LAST, 15, st_score(LAST, 15, 3), None)
            turn_heads(1, SM_LAST["tail"] % 2, 2 * LAST + 2, SM_LAST["tail"] - 1)


def kernel(L0_attn_x, L0_attn_wq, L0_attn_bq, L0_attn_wk, L0_attn_bk, L0_attn_wv, L0_attn_bv,
           L0_ffn_W, L0_ffn_b, L0_ffn_A, L0_ffn_B, L0_ffn_p_scores):
    import concourse.bacc as bacc
    from concourse.bass_utils import run_bass_kernel_spmd

    def rows(a):
        a = np.asarray(a)
        a = a.reshape(*a.shape[:-1], -1, KV, D)[..., ROW_ORDER]
        return np.moveaxis(a, -1, -2).reshape(*a.shape[:-3], -1)

    def columns(a):
        own = a.reshape(-1, D, KV)
        partner = own.reshape(-1, D // 2, 2, KV)[:, :, ::-1].reshape(own.shape)
        return np.stack([own, partner], -1).reshape(-1, P, 2)

    inv_freq = np.float32(1.0) / np.float32(10000.0) ** (np.arange(0, D, 2, dtype=np.float32) / np.float32(D))
    ang = np.arange(S, dtype=np.float32)[:, None] * inv_freq[None, :]
    sign = np.array([-1.0 if d < D // 2 else 1.0 for d in ROW_ORDER], np.float32)
    pair = [d % (D // 2) for d in ROW_ORDER]
    cosT = np.repeat(np.cos(ang).T[pair], KV, axis=0)
    sinT = np.repeat(np.sin(ang).T[pair] * sign[:, None], KV, axis=0)

    f = {
        "x": np.asarray(L0_attn_x).reshape(S, E),
        "wq": rows(L0_attn_wq),
        "wk": rows(L0_attn_wk),
        "wv": np.asarray(L0_attn_wv),
        "biases": np.concatenate([columns(rows(L0_attn_bq)), columns(rows(L0_attn_bk))]).transpose(1, 0, 2),
        "bv": np.asarray(L0_attn_bv),
        "wT": np.asarray(L0_ffn_W).T,
        "b": np.asarray(L0_ffn_b),
        "A": np.asarray(L0_ffn_A).transpose(1, 0, 2).reshape(E, RANK),
        "B": np.asarray(L0_ffn_B).reshape(RANK, E),
        "p_sc": np.repeat(np.asarray(L0_ffn_p_scores), RANK // len(L0_ffn_p_scores))[:, None],
        "cosT": cosT.astype(np.float32),
        "sinT": sinT.astype(np.float32),
        "ident": np.eye(P, dtype=np.float32),
        "ones": np.ones((KM - KR, KV, S), np.float32).astype(mybir.dt.np(BF16)),
        "identb": np.eye(P, dtype=np.float32).astype(mybir.dt.np(BF16)),
    }
    nc = bacc.Bacc("TRN2", target_bir_lowering=False, num_devices=1)
    arrays = {f"in_{k}": np.ascontiguousarray(v) for k, v in f.items()}
    args = {k: nc.dram_tensor(f"in_{k}", v.shape, mybir.dt.from_np(v.dtype), kind="ExternalInput").ap()
            for k, v in ((k, arrays[f"in_{k}"]) for k in f)}
    out = nc.dram_tensor("out", (S, E), F32, kind="ExternalOutput").ap()
    build(nc, out=out, **args)
    r = run_bass_kernel_spmd(nc, [arrays], core_ids=[0])
    return r.results[0]["out"].reshape(1, S, E)
```

```python
from contextlib import ExitStack

import numpy as np

import concourse.bass as bass
from concourse import mybir
from concourse.alu_op_type import AluOpType as ALU

F32 = mybir.dt.float32
BF16 = mybir.dt.bfloat16
ACT = mybir.ActivationFunctionType
AX = mybir.AxisListType

P = 128
S = 1024
E = 512
H, KV = 32, 8
D = E // H
REP = H // KV
NT = S // P
NE = E // P
HALF = S // 2
TH = NT // 2
CHUNKS = H // KV
RANK = 128
PARTS = 3
Q_SLOTS = (0, 1, 0, 1, 0, 2)
K_SLOTS = (0, 0, 1, 1, 2, 0)
KR = D * len(Q_SLOTS)
KM = KR + 2
VC = 32
PB = 4
ROW_ORDER = [j // 2 + (D // 2) * (j % 2) for j in range(D)]
PARTNER = [i ^ 8 for i in range(32)]
C_CLAMP, EPS_LN, EPS_M = 0.5, 1e-5, 1e-6

PJ = ([("xT", t, "act") for t in range(4)]
      + [("k", 0, "dve"), ("xT", 4, "act"), ("xT", 5, "act"), ("q", (0, 0), "dve"), ("xT", 6, "act"), ("xT", 7, "act"),
         ("k", 1, "dve"), ("q", (0, 1), "dve"), ("v", 0, "dve"), ("v", 1, "dve")])
MIXED = [("q", (1, 0), 0), ("q", (1, 1), 3), ("u", 0, 4), ("q", (2, 0), 3), ("u", 1, 4), ("q", (2, 1), 3), ("z", 0, 3),
         ("q", (3, 0), 2), ("z", 1, 3), ("q", (3, 1), 2), ("z", 2, 3), ("z", 3, 2)]
for _kind, _i, _rows in MIXED:
    if _kind == "z":
        PJ += [("m", _i, "act")]
    PJ += [(_kind, _i, "act" if _kind == "u" else "dve")]
    if (_kind, _i) == ("z", 1):
        PJ += [("max0", 0, "act")]
PJ_AT = {(kind, i): n for n, (kind, i, _) in enumerate(PJ)}


def emptied(n):
    who = PJ[n][2]
    return who, sum(w == who for _, _, w in PJ[:n + 1])


ST_PER, SM_PER = 66, 34
MAX1_SLOT, MAX0_SLOT = 2, 10
OUT1_SLOT, OUT0_SLOT = 2, 10


def st_score(g, s, h):
    return ST_PER * g + 4 * s + h + (s >= MAX1_SLOT) + (s >= MAX0_SLOT)


def st_max1(g):
    return ST_PER * g + 4 * MAX1_SLOT


def st_max0(g):
    return ST_PER * g + 4 * MAX0_SLOT + 1


def sm_base(g):
    return 31 + SM_PER * g


def sm_score(g, e, first=False):
    return sm_base(g) + e + (1 if e >= 2 * OUT1_SLOT else 0) + (1 if e >= 2 * OUT0_SLOT else 0) \
        + (1 if first and e < 2 * OUT1_SLOT else 0)


def sm_out1(g):
    return sm_base(g) + 2 * OUT1_SLOT


def sm_out0(g):
    return sm_base(g) + 2 * OUT0_SLOT + 1


LAST = KV - 1
SM_LAST = {what: sm_base(LAST) + i for i, what in enumerate((4, "out1", 5, 6, "out0", 7, "tail"))}
LATE_UNITS = {0: [(4, 0), (4, 1)], 1: [(4, 2), (4, 3), (4, NE)], 3: [(5, 0), (5, 1)], 4: [(5, 2), (5, 3)],
              5: [(5, NE), (6, 0)], 6: [(6, 1), (6, 2)], 7: [(6, 3), (6, NE)], 9: [(7, 0)],
              11: [(7, 1)], 12: [(7, 2), (7, 3)], 13: [(7, NE)]}


def build(nc, x, wq, wk, wv, biases, bv, wT, b, A, B, p_sc, cosT, sinT, ident, identb, ones, out):
    ctx = ExitStack()
    with ctx:
        def sb(name, shape, dt=F32):
            return ctx.enter_context(nc.sbuf_tensor(name, shape, dt))

        def sem(name):
            return ctx.enter_context(nc.semaphore(name))

        x_sb = sb("x_sb", [P, NT, E])
        n_parts = 3 * PARTS * HALF // 2
        arena = sb("arena", [P, n_parts + 2 * HALF * 2 + NE * E + 2 * S])
        probs = arena[:, 0:PB * REP * HALF].rearrange("p (b h n) -> p b h n", b=PB, h=REP)

        def piece(start, *shape):
            letters = "abcd"[:len(shape)]
            return arena[:, start:start + int(np.prod(shape))].rearrange(
                f"p ({' '.join(letters)}) -> p {' '.join(letters)}", **dict(zip(letters, shape)))

        wq_sb = piece(0, NE, E)
        tables = piece(NE * E, 2, S)
        rot = piece(NE * E + 2 * S, 2, HALF)
        swp = piece(NE * E + 2 * S + 2 * HALF, 2, HALF)
        parts_at = NE * E + 2 * S + 4 * HALF
        parts = arena[:, parts_at:parts_at + n_parts].bitcast(BF16).rearrange(
            "p (b k n) -> p b k n", b=3, k=PARTS)
        cos_sb, sin_sb = tables[:, 0, :], tables[:, 1, :]
        xT_sb = sb("xT_sb", [P, 2 * NE * HALF])
        xT = xT_sb[:, :].rearrange("p (h c n) -> p h c n", h=2, c=NE)
        late_gate = xT_sb[:, 0:NE * HALF].rearrange("p (t n) -> p t n", t=TH)
        wT_sb = sb("wT_sb", [P, NE, E])
        xn = sb("xn", [P, 2, E])
        wkv = sb("wkv", [P, 2, NE, P])
        wk_sb, wv_sb = wkv[:, 0, :, :], wkv[:, 1, :, :]
        heads = wkv[:, :, :, :].rearrange("p a c n -> p a (c n)")
        gated = sb("gated", [P, TH, REP * D])
        A_sb = sb("A_sb", [P, NE, RANK])
        B_sb = sb("B_sb", [RANK, E])
        uT = sb("uT", [RANK, S])
        qA = sb("qA", [KM, 2, KV, REP, HALF], BF16)
        kA = sb("kA", [KM, KV, S], BF16)
        z_sb = sb("z_sb", [P, TH, E])
        late_heads = sb("late_heads", [P, TH, E])
        m_sb = sb("m_sb", [P, 3, E])
        junk = sb("junk", [P, 2, E], BF16)
        zeros = junk[:, 0, :]
        v_sb = sb("v_sb", [P, NT, KV * D])
        vg = sb("vg", [P, NT, VC])
        id_sb = sb("id_sb", [P, P])
        idb_sb = sb("idb_sb", [P, P], BF16)
        b_sb = sb("b_sb", [P, E])
        bv_sb = sb("bv_sb", [P, KV * D])
        bias = sb("bias", [P, CHUNKS + 1, 2])
        p_sb = sb("p_sb", [RANK, 1])
        stats = sb("stats", [P, NT, 6])
        mv = sb("mv", [P, NT, 2])
        rstd = sb("rstd", [P, NT])
        consts = sb("consts", [P, 4])
        norms = sb("norms", [P, NT, 2])
        gam = sb("gam", [P, NT, 2])
        negmax = sb("negmax", [P, 2, 16])
        maxp = sb("maxp", [P, 2, 32], BF16)
        maxT = sb("maxT", [32, 2, P], BF16)
        rsum = sb("rsum", [P, TH * REP])
        scaled = sb("scaled", [P, TH, REP * D])

        sm = ctx.enter_context(nc.psum_tensor("sm", [P, 2, S], F32))
        st = ctx.enter_context(nc.psum_tensor("st", [P, 3, HALF], F32))
        oT = ctx.enter_context(nc.psum_tensor("oT", [P, HALF], F32))

        def pj(n):
            return oT[:, :] if n % 4 == 3 else st[:, n % 4, :]

        x_in = [sem(f"x_in{t}") for t in range(NT)]
        wk_in, wq0_in, wq_in, wv_in, tab_in, ffn_in, small_in = (sem(n) for n in (
            "wk_in", "wq0_in", "wq_in", "wv_in", "tab_in", "ffn_in", "small_in"))
        id_in, ones_in = sem("id_in"), sem("ones_in")
        zeros_set = sem("zeros_set")
        const_set = sem("const_set")
        stats_done, mean_var, eps_added, rstd_done = (sem(n) for n in (
            "stats_done", "mean_var", "eps_added", "rstd_done"))
        xn_done = sem("xn_done")
        pj_full, pj_act, pj_dve = sem("pj_full"), sem("pj_act"), sem("pj_dve")
        cos_mul, swapped, sin_mul = sem("cos_mul"), sem("swapped"), sem("sin_mul")
        rotated, part1, left1, part2, part3 = (sem(n) for n in ("rotated", "part1", "left1", "part2", "part3"))
        stacked = [sem(f"stacked{n}") for n in range(2 + 2 * CHUNKS)]
        norm_done, pow_step, gamma_done = sem("norm_done"), sem("pow_step"), sem("gamma_done")
        gate_in, gate_tanh, gate_done = sem("gate_in"), sem("gate_tanh"), sem("gate_done")
        sm_full, sm_free = sem("sm_full"), sem("sm_free")
        st_full, st_free = sem("st_full"), sem("st_free")
        max_hi, max_parts, max_in = sem("max_hi"), sem("max_parts"), sem("max_in")
        v_ready, pv_done = sem("v_ready"), sem("pv_done")
        heads_out, sums_inv, heads_scaled, heads_gated, group_done = (sem(n) for n in (
            "heads_out", "sums_inv", "heads_scaled", "heads_gated", "group_done"))
        late_copied, late_scaled, late_added = sem("late_copied"), sem("late_scaled"), sem("late_added")
        last_gated, stored = sem("last_gated"), sem("stored")

        halves = [(kind, i) for kind, i, _ in PJ if kind in "kq"]

        def dense(t):
            return z_sb[:, t, :] if t < TH else late_gate[:, t - TH, :]

        LATE = (KV - 1) * REP * D

        block = ctx.enter_context(nc.Block())

        @block.sync
        def _(sp):
            for t in range(NT):
                sp.dma_start(x_sb[:, t, :], x[t * P:(t + 1) * P, :]).then_inc(x_in[t], 16)
            wq_v = wq.rearrange("(c p) n -> p c n", p=P)
            sp.dma_start(wv_sb, wv.rearrange("(c p) n -> p c n", p=P)).then_inc(wv_in, 16)
            sp.dma_start(wq_sb[:, :, P:E], wq_v[:, :, P:E]).then_inc(wq_in, 16)
            sp.dma_start(A_sb[:, :, :], A.rearrange("(c p) n -> p c n", p=P)).then_inc(ffn_in, 16)
            sp.dma_start(p_sb[:, :], p_sc).then_inc(ffn_in, 16)
            sp.dma_start(idb_sb[:, :], identb).then_inc(small_in, 16)
            sp.dma_start(kA[KR:KM, :, :], ones).then_inc(ones_in, 16)
            sp.dma_start(bv_sb[:, :], bv.partition_broadcast(P)).then_inc(wv_in, 16)
            sp.dma_start(wT_sb[:, :, :], wT.rearrange("(c p) n -> p c n", p=P)).then_inc(ffn_in, 16)
            sp.dma_start(B_sb[:, :], B).then_inc(ffn_in, 16)
            sp.dma_start(b_sb[:, :], b.partition_broadcast(P)).then_inc(ffn_in, 16)

            def maxima_row(g, half):
                sp.dma_start(qA[KR:KM, half, bass.ds(g, 1), :, :].rearrange("p a h (r c) -> p (a h r) c", c=P),
                             maxT[:, half, :]).then_inc(max_in, 16)

            for n, (kind, i) in enumerate(halves):
                if n == len(halves) - 1:
                    sp.wait_ge(pj_act, emptied(PJ_AT["max0", 0])[1])
                    maxima_row(0, 0)
                of_slot = K_SLOTS if kind == "k" else Q_SLOTS
                for slot in sorted(range(len(of_slot)), key=lambda k: of_slot[k]):
                    sp.wait_ge((part1, part2, part3)[of_slot[slot]], n + 1)
                    rows = slice(slot * D, (slot + 1) * D)
                    if kind == "k":
                        sp.dma_start(kA[rows, :, i * HALF:(i + 1) * HALF],
                                     parts[:, n % 3, of_slot[slot], :]).then_inc(stacked[n], 16)
                    else:
                        c, hh = i
                        sp.dma_start(qA[rows, hh, 2 * c:2 * c + 2, :, :].rearrange("d a h n -> d (a h) n"),
                                     parts[:, n % 3, of_slot[slot], :]).then_inc(stacked[n], 16)

            def step(g, more):
                sp.wait_ge(st_free, st_max1(g) + 1)
                sp.wait_ge(max_in, 16 * (2 * g + 1))
                maxima_row(g, 1)
                if more:
                    sp.wait_ge(st_free, st_max0(g) + 1)
                    sp.wait_ge(max_in, 16 * (2 * g + 2))
                    maxima_row(g + 1, 0)

            step(0, True)
            with sp.Fori(1, LAST) as g:
                step(g, True)
            step(LAST, False)
            o_t = out.rearrange("(t p) n -> p t n", p=P)
            sp.wait_ge(group_done, KV - 1)
            sp.dma_start(o_t[:, 0:TH, 0:LATE], x_sb[:, 0:TH, 0:LATE]).then_inc(stored, 16)
            for t in range(TH, NT):
                if t == NT - 1:
                    sp.wait_ge(group_done, KV)
                    sp.dma_start(o_t[:, 0:TH, LATE:E], x_sb[:, 0:TH, LATE:E]).then_inc(stored, 16)
                sp.wait_ge(late_added, t - TH + 1)
                sp.dma_start(o_t[:, t, 0:LATE], x_sb[:, t, 0:LATE]).then_inc(stored, 16)
            sp.wait_ge(group_done, KV + 1)
            sp.dma_start(o_t[:, TH:NT, LATE:E], x_sb[:, TH:NT, LATE:E]).then_inc(stored, 16)
            sp.wait_ge(stored, 16 * (TH + 3))

        @block.gpsimd
        def _(pool):
            for n, v in enumerate((-0.5, 0.5, -1.0, 0.0)):
                pool.memset(consts[:, n:n + 1], v).then_inc(const_set, 1)
            pool.memset(vg[:, :, D + 1:VC], 0.0).then_inc(const_set, 1)
            pool.memset(vg[:, :, D:D + 1], 2.0).then_inc(const_set, 1)
            pool.wait_ge(const_set, 6)
            for t in range(NT):
                pool.wait_ge(mean_var, t + 1)
                pool.tensor_scalar(mv[:, t, 1:2], mv[:, t, 1:2], EPS_LN, None, ALU.add).then_inc(eps_added, 1)
                pool.wait_ge(eps_added, t + 1)
                pool.tensor_tensor(rstd[:, t:t + 1], mv[:, t, 1:2], consts[:, 0:1], ALU.pow).then_inc(rstd_done, 1)

            def rope_sum(n):
                pool.wait_ge(sin_mul, n + 1)
                pool.tensor_tensor(rot[:, n % 2, :], rot[:, n % 2, :], swp[:, n % 2, :], ALU.add).then_inc(rotated, 1)

            def left_over(n):
                pool.wait_ge(part1, n + 1)
                pool.tensor_tensor(rot[:, n % 2, :], rot[:, n % 2, :], parts[:, n % 3, 0, :],
                                   ALU.subtract).then_inc(left1, 1)

            def third_part(n):
                pool.wait_ge(part2, n + 1)
                pool.tensor_tensor(parts[:, n % 3, 2, :], rot[:, n % 2, :], parts[:, n % 3, 1, :],
                                   ALU.subtract).then_inc(part3, 1)

            rope_sum(0)
            for n in range(len(halves) - 2):
                left_over(n)
                if n < 2:
                    rope_sum(n + 1)
                third_part(n)
                if 2 <= n < len(halves) - 3:
                    rope_sum(n + 1)

            def split(n):
                rope_sum(n)
                left_over(n)
                third_part(n)

            def gamma(t):
                pool.wait_ge(norm_done, 2 * t + 2)
                pool.tensor_tensor(gam[:, t, :], norms[:, t, :], consts[:, 1:2].broadcast_to((P, 2)),
                                   ALU.pow).then_inc(pow_step, 1)
                pool.wait_ge(pow_step, 4 * t + 1)
                pool.tensor_scalar(gam[:, t, 1:2], gam[:, t, 1:2], EPS_M, None, ALU.add).then_inc(pow_step, 1)
                pool.wait_ge(pow_step, 4 * t + 2)
                pool.tensor_tensor(gam[:, t, 1:2], gam[:, t, 1:2], consts[:, 2:3], ALU.pow).then_inc(pow_step, 1)
                pool.wait_ge(pow_step, 4 * t + 3)
                pool.tensor_tensor(gam[:, t, 0:1], gam[:, t, 0:1], gam[:, t, 1:2], ALU.mult).then_inc(pow_step, 1)
                pool.wait_ge(pow_step, 4 * t + 4)
                pool.tensor_scalar(gam[:, t, 0:1], gam[:, t, 0:1], C_CLAMP, 1.0, ALU.mult,
                                   ALU.min).then_inc(gamma_done, 1)

            def maxima(half, count, filled, emptied_by):
                pool.wait_ge(sm_free, filled)
                if emptied_by is not None:
                    pool.wait_ge(*emptied_by)
                pool.tensor_tensor(maxp[:, half, 0:16], negmax[:, half, :], consts[:, 3:4].broadcast_to((P, 16)),
                                   ALU.add).then_inc(max_hi, 1)
                pool.wait_ge(max_hi, count)
                pool.tensor_tensor(maxp[:, half, 16:32], negmax[:, half, :], maxp[:, half, 0:16],
                                   ALU.subtract).then_inc(max_parts, 1)

            def group_values(g):
                cols = bass.ds(g * D, D)
                pool.tensor_tensor(vg[:, :, 0:D], v_sb[:, :, cols],
                                   bv_sb[:, cols].unsqueeze(1).broadcast_to((P, NT, D)), ALU.add).then_inc(v_ready, 1)

            maxima(0, 1, 16, None)
            gamma(0)
            split(len(halves) - 2)
            gamma(1)
            split(len(halves) - 1)
            pool.wait_ge(pj_dve, emptied(PJ_AT["v", 1])[1])
            pool.wait_ge(wv_in, 32)
            group_values(0)
            gamma(2)
            gamma(3)
            maxima(1, 2, 32, None)

            def finish(g, half, n, gate_at):
                pool.wait_ge(heads_scaled, 2 * g + half + 1)
                cols = bass.ds(g * (REP * D), REP * D)
                ts = slice(half * TH, (half + 1) * TH)
                pool.tensor_tensor(gated[:, :, :], scaled[:, :, :], gate_at[:, :, cols],
                                   ALU.mult).then_inc(heads_gated, 1)
                pool.wait_ge(heads_gated, n + 1)
                pool.tensor_tensor(x_sb[:, ts, cols], x_sb[:, ts, cols], gated[:, :, :],
                                   ALU.add).then_inc(group_done, 1)

            def step(g, first=False):
                if not first:
                    pool.wait_ge(pv_done, 16 * g)
                    group_values(g)
                maxima(0, 2 * g + 3, sm_score(g, 15) + 1,
                       (pj_full, PJ_AT["max0", 0] + 1) if first else (st_full, st_max0(g - 1) + 1))
                if first:
                    pool.wait_ge(gate_done, TH)
                finish(g, 0, g, z_sb)
                maxima(1, 2 * g + 4, sm_score(g, 31) + 1, (st_full, st_max1(g) + 1))

            step(0, first=True)
            with pool.Fori(1, LAST) as g:
                step(g)

            def add_late(t):
                pool.wait_ge(gate_done, t + 1)
                held = late_heads[:, t - TH, 0:LATE]
                pool.tensor_tensor(held, held, late_gate[:, t - TH, 0:LATE], ALU.mult).then_inc(late_scaled, 1)
                pool.wait_ge(late_scaled, t - TH + 1)
                pool.tensor_tensor(x_sb[:, t, 0:LATE], x_sb[:, t, 0:LATE], held, ALU.add).then_inc(late_added, 1)

            pool.wait_ge(pv_done, 16 * LAST)
            group_values(LAST)
            gamma(4)
            gamma(5)
            add_late(4)
            gamma(6)
            add_late(5)
            finish(LAST, 0, LAST, z_sb)
            add_late(6)
            gamma(7)
            add_late(7)

        @block.scalar
        def _(act):
            act.dma_start(id_sb[:, :], ident).then_inc(id_in, 16)
            act.dma_start(wk_sb, wk.rearrange("(c p) n -> p c n", p=P)).then_inc(wk_in, 16)
            act.dma_start(wq_sb[:, :, 0:P], wq.rearrange("(c p) n -> p c n", p=P)[:, :, 0:P]).then_inc(wq0_in, 16)
            act.dma_start(bias[:, :, :], biases).then_inc(small_in, 16)
            act.dma_start(cos_sb, cosT).then_inc(tab_in, 16)
            act.dma_start(sin_sb, sinT).then_inc(tab_in, 16)

            for t in range(NT):
                act.wait_ge(pj_full, PJ_AT["xT", t] + 1)
                act.activation(xT[:, t // TH, :, t % TH * P:(t % TH + 1) * P],
                               pj(PJ_AT["xT", t]).rearrange("p (c n) -> p c n", c=NE), ACT.Copy).then_inc(pj_act, 1)

            def cast(n):
                act.wait_ge(rotated, n + 1)
                if n >= 3:
                    act.wait_ge(stacked[n - 3], 16 * len(Q_SLOTS))
                act.activation(parts[:, n % 3, 0, :], rot[:, n % 2, :], ACT.Copy).then_inc(part1, 1)
                act.wait_ge(left1, n + 1)
                act.activation(parts[:, n % 3, 1, :], rot[:, n % 2, :], ACT.Copy).then_inc(part2, 1)

            for n in range(len(halves) - 2):
                cast(n)
                if n in (5, 6):
                    hh = n - 5
                    e = PJ_AT["u", hh]
                    act.wait_ge(ffn_in, 80)
                    act.wait_ge(pj_full, e + 1)
                    act.activation(uT[:, hh * HALF:(hh + 1) * HALF], pj(e), ACT.Copy,
                                   scale=p_sb[:, 0:1]).then_inc(pj_act, 1)

            def gate_tanh_of(t):
                act.wait_ge(gate_in, t + 1)
                act.activation(m_sb[:, t % 3, :], dense(t), ACT.Tanh, scale=0.5).then_inc(gate_tanh, 1)

            def squares(t):
                n = PJ_AT["m", t]
                act.wait_ge(pj_full, n + 1)
                if t >= 3:
                    act.wait_ge(gate_done, t - 2)
                if t >= 1:
                    act.wait_ge(norm_done, 2 * t)
                act.activation(junk[:, 1, :], pj(n), ACT.Square,
                               accum_out=norms[:, t, 1:2]).then_inc(norm_done, 1)
                act.activation(m_sb[:, t % 3, :], pj(n), ACT.Copy).then_inc(pj_act, 1)
                act.wait_ge(pj_dve, emptied(PJ_AT["z", t])[1])
                act.activation(junk[:, 0, :], z_sb[:, t, :], ACT.Square,
                               accum_out=norms[:, t, 0:1]).then_inc(norm_done, 1)

            squares(0)
            gate_tanh_of(0)
            cast(len(halves) - 2)
            squares(1)
            act.wait_ge(pj_full, PJ_AT["max0", 0] + 1)
            act.activation(maxT[:, 0, :], pj(PJ_AT["max0", 0]).bitcast(BF16)[0:32, 0:P], ACT.Copy).then_inc(pj_act, 1)
            gate_tanh_of(1)
            cast(len(halves) - 1)
            squares(2)
            squares(3)

            def evacuate(g, half, n, free):
                act.wait_ge(pv_done, 16 * g + 8 * (half + 1))
                if free is not None:
                    act.wait_ge(sm_full, free)
                act.activation(heads[:, half, :], oT[:, :], ACT.Copy).then_inc(heads_out, 1)

            def step(g, first=False, last=False):
                for s in range(16):
                    if s == MAX1_SLOT:
                        act.wait_ge(st_full, st_max1(g) + 1)
                        if not first:
                            act.wait_ge(max_in, 16 * 2 * g)
                        act.activation(maxT[:, 1, :], st[:, st_max1(0) % 3, :].bitcast(BF16)[0:32, 0:P],
                                       ACT.Copy).then_inc(st_free, 1)
                    if s == MAX0_SLOT and not last:
                        act.wait_ge(st_full, st_max0(g) + 1)
                        act.wait_ge(max_in, 16 * (2 * g + 1))
                        act.activation(maxT[:, 0, :], st[:, st_max0(0) % 3, :].bitcast(BF16)[0:32, 0:P],
                                       ACT.Copy).then_inc(st_free, 1)
                    for h in range(REP):
                        fewer = 1 if last and s >= MAX0_SLOT else 0
                        act.wait_ge(st_full, st_score(g, s, h) + 1 - fewer)
                        if h == 0 and not (first and s < PB):
                            act.wait_ge(pv_done, 16 * g + s - PB + 1)
                        if first and h == 0 and s in (1, 2):
                            act.wait_ge(part3, len(halves))
                        if first and h == 0 and s == 3:
                            for n in range(len(halves) - 2, len(halves)):
                                act.wait_ge(stacked[n], 16 * len(Q_SLOTS))
                        act.activation(probs[:, s % PB, h, :], st[:, (st_score(0, s, h) - fewer) % 3, :], ACT.Exp,
                                       scale=float(D) ** -0.5).then_inc(st_free, 1)
                        if first and (s, h) in ((1, 3), (3, 3)):
                            gate_tanh_of({1: 2, 3: 3}[s])
                        if last and (s, h) in ((3, 3), (7, 3), (10, 3), (15, 3)):
                            gate_tanh_of({3: 4, 7: 5, 10: 6, 15: 7}[s])
                        if s == 0 and h == 2 and not first:
                            evacuate(g - 1, 1, 2 * g - 1, sm_base(g - 1) + 2 * OUT1_SLOT + 1)
                        if s == 8 and h == 2:
                            evacuate(g, 0, 2 * g, None if first else sm_out0(g - 1) + 1)

            step(0, first=True)
            with act.Fori(1, LAST) as g:
                step(g)
            step(LAST, last=True)
            evacuate(LAST, 1, 2 * LAST + 1, SM_LAST["out1"] + 1)

        @block.vector
        def _(dve):
            def normalise(t):
                dve.wait_ge(rstd_done, t + 1)
                if t >= 2:
                    dve.wait_ge(pj_full, PJ_AT["xT", t - 2] + 1)
                dve.tensor_scalar(xn[:, t % 2, :], x_sb[:, t, :], mv[:, t, 0:1], rstd[:, t:t + 1],
                                  ALU.subtract, ALU.mult).then_inc(xn_done, 1)

            dve.memset(zeros, 0.0).then_inc(zeros_set, 1)
            for t in range(NT):
                dve.wait_ge(x_in[t], 16)
                dve.bn_stats(stats[:, t, :], x_sb[:, t, :]).then_inc(stats_done, 1)
                dve.wait_ge(stats_done, t + 1)
                dve.bn_aggr(mv[:, t, :], stats[:, t, :]).then_inc(mean_var, 1)
                if t >= 1:
                    normalise(t - 1)
            normalise(NT - 1)

            def rope(kind, i):
                n = halves.index((kind, i))
                col = CHUNKS if kind == "k" else i[0]
                hh = i if kind == "k" else i[1]
                e = PJ_AT[kind, i]
                tok = slice(hh * HALF, (hh + 1) * HALF)
                dve.wait_ge(pj_full, e + 1)
                if n >= 2:
                    dve.wait_ge(part3, n - 1)
                dve.scalar_tensor_tensor(rot[:, n % 2, :], pj(e), bias[:, col, 0:1], cos_sb[:, tok],
                                         ALU.add, ALU.mult).then_inc(cos_mul, 1)
                dve.stream_shuffle(swp[:, n % 2, :], pj(e), PARTNER).then_inc(pj_dve, 1)
                dve.wait_ge(pj_dve, emptied(e)[1])
                dve.scalar_tensor_tensor(swp[:, n % 2, :], swp[:, n % 2, :], bias[:, col, 1:2], sin_sb[:, tok],
                                         ALU.add, ALU.mult).then_inc(sin_mul, 1)

            dve.wait_ge(small_in, 32)
            dve.wait_ge(tab_in, 32)
            for kind, i in halves[:4]:
                rope(kind, i)
            for hh in range(2):
                e = PJ_AT["v", hh]
                dve.wait_ge(pj_full, e + 1)
                dve.tensor_copy(v_sb[:, hh * TH:(hh + 1) * TH, :],
                                pj(e).rearrange("p (t n) -> p t n", t=TH)).then_inc(pj_dve, 1)

            def row_max(n_full, bank, half, r, parts_done):
                dve.wait_ge(sm_full, n_full)
                if parts_done is not None:
                    dve.wait_ge(max_parts, parts_done)
                dve.tensor_reduce(negmax[:, half, r:r + 1], sm[:, bank, :], AX.X, ALU.max,
                                  negate=True).then_inc(sm_free, 1)

            def gate_sum(t):
                dve.wait_ge(gamma_done, t + 1)
                if t < TH:
                    dve.wait_ge(pj_act, emptied(PJ_AT["m", t])[1])
                dve.scalar_tensor_tensor(dense(t), m_sb[:, t % 3, :], gam[:, t, 0:1], dense(t),
                                         ALU.mult, ALU.add).then_inc(gate_in, 1)

            def gate(t):
                dve.wait_ge(gate_tanh, t + 1)
                dve.scalar_tensor_tensor(dense(t), m_sb[:, t % 3, :], 1.0, dense(t),
                                         ALU.add, ALU.mult).then_inc(gate_done, 1)

            gate_work = {("q", (3, 0), 1): (gate_sum, 0), ("z", 1, 0): (gate, 0),
                         ("q", (3, 1), 1): (gate_sum, 1), ("z", 2, 0): (gate, 1)}
            n = 0
            for kind, i, rows in MIXED:
                if (kind, i) == ("z", 0):
                    dve.wait_ge(ffn_in, 80)
                for r in range(rows):
                    row_max(n + 1, n % 2, n // 16, n % 16, None)
                    n += 1
                    if (kind, i, r) in gate_work:
                        stage, t = gate_work[kind, i, r]
                        stage(t)
                if kind == "q":
                    rope("q", i)
                if kind == "z":
                    e = PJ_AT["z", i]
                    dve.wait_ge(pj_full, e + 1)
                    dve.tensor_tensor(z_sb[:, i, :], pj(e), b_sb[:, :], ALU.add).then_inc(pj_dve, 1)

            def scale_heads(n_full, bank, n, to, done):
                turned = sm[:, bank, 0:HALF].rearrange("p (t h c) -> p t h c", t=TH, h=REP)
                dve.wait_ge(sm_full, n_full)
                if done is not None:
                    dve.wait_ge(group_done, done)
                dve.reciprocal(rsum[:, :].rearrange("p (t h) -> p t h", t=TH), turned[:, :, :, D]).then_inc(sums_inv, 1)
                dve.wait_ge(sums_inv, n + 1)
                dve.tensor_tensor(to.rearrange("p t (h d) -> p t h d", h=REP), turned[:, :, :, 0:D],
                                  rsum[:, :].rearrange("p (t h) -> p t h", t=TH).unsqueeze(3)
                                  .broadcast_to((P, TH, REP, D)), ALU.mult).then_inc(heads_scaled, 1)
                dve.wait_ge(heads_scaled, n + 1)
                dve.sem_inc(sm_free, 1)

            def hold_heads(g, n_full, bank):
                scale_heads(n_full, bank, 2 * g + 1, late_heads[:, :, bass.ds(g * (REP * D), REP * D)], None)

            def step(g, first=False):
                for e in range(32):
                    if e == 2 * OUT1_SLOT and not first:
                        hold_heads(g - 1, sm_out1(g) + 1, sm_out1(0) % 2)
                    if e == 2 * OUT0_SLOT:
                        scale_heads(sm_out0(g) + 1, sm_out0(0) % 2, 2 * g, scaled[:, :, :], None if first else g)
                    row_max(sm_score(g, e, first) + 1, sm_score(0, e, first) % 2, e // 16, e % 16,
                            2 * g + e // 16 + 1 if e % 16 == 0 else None)
                    if first and e in (0, 3):
                        gate_sum({0: 2, 3: 3}[e])
                    if first and e == 5:
                        gate(2)
                    if first and e == 9:
                        gate(3)

            step(0, first=True)
            with dve.Fori(1, LAST) as g:
                step(g)

            def late_dense(t):
                n = SM_LAST[t]
                unread = uT[:, 0:HALF]
                dve.wait_ge(sm_full, n + 1)
                dve.tensor_tensor(dense(t), sm[:, n % 2, 0:HALF], b_sb[:, :], ALU.add).then_inc(late_copied, 1)
                dve.wait_ge(gate_done, t - 2)
                dve.tensor_copy(m_sb[:, t % 3, :], sm[:, n % 2, HALF:S]).then_inc(late_copied, 1)
                dve.wait_ge(late_copied, 2 * (t - TH) + 2)
                dve.sem_inc(sm_free, 1)
                for k, values in ((1, m_sb[:, t % 3, :]), (0, dense(t))):
                    dve.wait_ge(norm_done, 2 * t + 1 - k)
                    dve.scalar_tensor_tensor(unread, values, 1.0, values, ALU.mult, ALU.mult,
                                             accum_out=norms[:, t, k:k + 1]).then_inc(norm_done, 1)

            late_dense(4)
            hold_heads(LAST - 1, SM_LAST["out1"] + 1, SM_LAST["out1"] % 2)
            gate_sum(4)
            late_dense(5)
            gate(4)
            gate_sum(5)
            late_dense(6)
            gate(5)
            gate_sum(6)
            scale_heads(SM_LAST["out0"] + 1, SM_LAST["out0"] % 2, 2 * LAST, scaled[:, :, :], LAST)
            gate(6)
            late_dense(7)
            gate_sum(7)
            gate(7)
            scale_heads(SM_LAST["tail"] + 1, SM_LAST["tail"] % 2, 2 * LAST + 1, scaled[:, :, :], LAST + 1)
            dve.tensor_tensor(scaled[:, :, :], scaled[:, :, :], late_gate[:, :, LATE:E],
                              ALU.mult).then_inc(last_gated, 1)
            dve.wait_ge(last_gated, 1)
            dve.tensor_tensor(x_sb[:, TH:NT, LATE:E], x_sb[:, TH:NT, LATE:E], scaled[:, :, :],
                              ALU.add).then_inc(group_done, 1)

        @block.tensor
        def _(pe):
            def claim(n):
                if n >= 4:
                    who, count = emptied(n - 4)
                    pe.wait_ge(pj_act if who == "act" else pj_dve, count)

            def project(kind, i, weight, columns, moving, rows=0):
                n = PJ_AT[kind, i]
                claim(n)
                for c in range(NE):
                    mm = pe.matmul(pj(n), weight[:, c, columns], moving[:, c, :], start=(c == 0), stop=(c == NE - 1))
                    if c == NE - 1:
                        mm.then_inc(pj_full, 1)
                    if c < rows:
                        next_maximum()

            def turn_tokens(t):
                n = PJ_AT["xT", t]
                pe.wait_ge(xn_done, t + 1)
                claim(n)
                for c in range(NE):
                    mm = pe.transpose(pj(n)[:, c * P:(c + 1) * P], xn[:, t % 2, c * P:(c + 1) * P], id_sb[:, :])
                mm.then_inc(pj_full, 1)

            def keep_warm(count):
                for _ in range(count):
                    pe.matmul(sm[:, 0, 0:HALF], zeros[:, 0:P], zeros[:, :], start=True, stop=True)

            pe.wait_ge(zeros_set, 1)
            keep_warm(13)
            pe.wait_ge(id_in, 16)
            for kind, i, _ in PJ[:PJ_AT["v", 0]]:
                if kind == "xT":
                    turn_tokens(i)
                    keep_warm(2 if i < TH else 0)
                elif kind == "k":
                    pe.wait_ge(wk_in, 16)
                    n = PJ_AT[kind, i]
                    claim(n)
                    for pair in range(2):
                        pe.wait_ge(pj_act, TH * i + 2 * pair + 2)
                        tok = slice(pair * 2 * P, (pair + 1) * 2 * P)
                        for c in range(NE):
                            mm = pe.matmul(pj(n)[:, tok], wk_sb[:, c, :], xT[:, i, c, tok],
                                           start=(c == 0), stop=(c == NE - 1))
                    mm.then_inc(pj_full, 1)
                else:
                    pe.wait_ge(wq0_in, 16)
                    project("q", i, wq_sb, slice(0, P), xT[:, i[1]])
            pe.wait_ge(wv_in, 32)
            for hh in range(2):
                n = PJ_AT["v", hh]
                claim(n)
                for t in range(TH):
                    for c in range(NE):
                        mm = pe.matmul(pj(n)[:, t * P:(t + 1) * P], xT[:, hh, c, t * P:(t + 1) * P], wv_sb[:, c, :],
                                       start=(c == 0), stop=(c == NE - 1))
                mm.then_inc(pj_full, 1)
            pe.wait_ge(wq_in, 16)

            def score_rows(g, e, n, bank, freed):
                half, h, qt = e // 16, (e % 16) // TH, e % TH
                if freed is not None:
                    pe.wait_ge(sm_free, freed)
                for kh in range(2):
                    mm = pe.matmul(sm[:, bank, kh * HALF:(kh + 1) * HALF],
                                   qA[0:KR, half, bass.ds(g, 1), h, qt * P:(qt + 1) * P]
                                   .rearrange("p a n -> p (a n)"),
                                   kA[0:KR, bass.ds(g, 1), kh * HALF:(kh + 1) * HALF].rearrange("p a n -> p (a n)"),
                                   start=True, stop=True)
                mm.then_inc(sm_full, 1)

            entries = iter(range(32))

            def next_maximum():
                e = next(entries)
                for n in {0: (0, 1, 2), 16: (3,)}.get(e, ()):
                    pe.wait_ge(stacked[n], 16 * len(Q_SLOTS))
                score_rows(0, e, e, e % 2, e - 1 if e >= 2 else None)

            def turn_maxima(out_bank, half):
                return pe.transpose(out_bank.bitcast(BF16)[0:32, 0:P], maxp[:, half, :], idb_sb[:, :])

            for kind, i, rows in MIXED:
                if kind == "q":
                    c, hh = i
                    project("q", i, wq_sb, slice(c * P, (c + 1) * P), xT[:, hh], rows)
                if (kind, i) == ("u", 0):
                    pe.wait_ge(ffn_in, 80)
                if kind == "u":
                    project("u", i, A_sb, slice(0, RANK), xT[:, i], rows)
                if kind == "z":
                    dense_tile = xT[:, i // TH, :, i % TH * P:(i % TH + 1) * P]
                    n = PJ_AT["m", i]
                    claim(n)
                    pe.wait_ge(pj_act, emptied(PJ_AT["u", i // TH])[1])
                    pe.matmul(pj(n), uT[:, i * P:(i + 1) * P], B_sb[:, :], start=True, stop=True).then_inc(pj_full, 1)
                    project("z", i, dense_tile, slice(0, P), wT_sb, rows)
                if (kind, i) == ("z", 1):
                    pe.wait_ge(small_in, 32)
                    n = PJ_AT["max0", 0]
                    claim(n)
                    pe.wait_ge(max_parts, 1)
                    turn_maxima(pj(n), 0).then_inc(pj_full, 1)
            pe.wait_ge(const_set, 6)
            pe.wait_ge(ones_in, 16)

            def claim_bank(bank):
                claim(4 + max(n for n in range(len(PJ)) if n % 4 == bank))

            for n in range(4, len(halves) - 2):
                pe.wait_ge(stacked[n], 16 * len(Q_SLOTS))

            def values(g, s, exps, free):
                kt = s % NT
                pe.wait_ge(st_free, exps)
                if kt == 0:
                    if free is None and s == 0:
                        claim_bank(3)
                    if free is not None:
                        pe.wait_ge(heads_out, free)
                    if s == 0:
                        pe.wait_ge(v_ready, g + 1)
                for h in range(REP):
                    mm = pe.matmul(oT[h * VC:(h + 1) * VC, :], vg[:, kt, :], probs[:, s % PB, h, :],
                                   start=(kt == 0), stop=(kt == NT - 1))
                mm.then_inc(pv_done, 1)

            def turn_heads(half, bank, n_heads, freed):
                pe.wait_ge(heads_out, n_heads)
                pe.wait_ge(sm_free, freed)
                for t in range(TH):
                    mm = pe.transpose(sm[:, bank, t * P:(t + 1) * P], heads[:, half, t * P:(t + 1) * P], id_sb[:, :])
                mm.then_inc(sm_full, 1)

            def late_unit(t, c):
                n = SM_LAST[t]
                if c == 0:
                    pe.wait_ge(sm_free, n - 1)
                if c < NE:
                    pe.matmul(sm[:, n % 2, 0:HALF], xT[:, 1, c, (t - TH) * P:(t - TH + 1) * P], wT_sb[:, c, :],
                              start=(c == 0), stop=(c == NE - 1))
                else:
                    pe.matmul(sm[:, n % 2, HALF:S], uT[:, t * P:(t + 1) * P], B_sb[:, :],
                              start=True, stop=True).then_inc(sm_full, 1)

            def step(g, first=False, last=False):
                for s in range(16):
                    half, kt = s // NT, s % NT
                    fewer = 1 if last and s >= MAX0_SLOT else 0

                    def score_cols(h):
                        n = st_score(g, s, h) - fewer
                        if first and s == 0 and h < 3:
                            claim_bank(h)
                        else:
                            pe.wait_ge(st_free, n - 2)
                        pe.matmul(st[:, (st_score(0, s, h) - fewer) % 3, :],
                                  kA[:, bass.ds(g, 1), kt * P:(kt + 1) * P].rearrange("p a n -> p (a n)"),
                                  qA[:, half, bass.ds(g, 1), h, :].rearrange("p a n -> p (a n)"),
                                  start=True, stop=True).then_inc(st_full, 1)

                    def next_rows(e):
                        if not last:
                            n = sm_score(g, e, first)
                            score_rows(g + 1, e, n, sm_score(0, e, first) % 2, n - 1)

                    if s == MAX1_SLOT:
                        pe.wait_ge(max_parts, 2 * g + 2)
                        pe.wait_ge(st_free, st_max1(g) - 2)
                        turn_maxima(st[:, st_max1(0) % 3, :], 1).then_inc(st_full, 1)
                    if s == MAX0_SLOT and not last:
                        pe.wait_ge(max_parts, 2 * g + 3)
                        pe.wait_ge(st_free, st_max0(g) - 2)
                        turn_maxima(st[:, st_max0(0) % 3, :], 0).then_inc(st_full, 1)
                    if s % NT == 0:
                        pe.wait_ge(max_in, 16 * (2 * g + half + 1))
                    score_cols(0)
                    if s == OUT1_SLOT and not first:
                        n = SM_LAST["out1"] if last else sm_out1(g)
                        turn_heads(1, (n if last else sm_out1(0)) % 2, 2 * g, n - 1)
                    if s == OUT0_SLOT:
                        n = SM_LAST["out0"] if last else sm_out0(g)
                        turn_heads(0, (n if last else sm_out0(0)) % 2, 2 * g + 1, n - 1)
                    if last:
                        units = list(LATE_UNITS.get(s, ()))
                    score_cols(1)
                    next_rows(2 * s)
                    if last and units:
                        late_unit(*units.pop(0))
                    score_cols(2)
                    if s > 0:
                        values(g, s - 1, st_score(g, s - 1, 3) + 1 - (1 if last and s - 1 >= MAX0_SLOT else 0),
                               None if first and s == 1 else 2 * g + (s - 1) // NT)
                    elif not first:
                        values(g - 1, 15, st_score(g - 1, 15, 3) + 1, None)
                    if last and units:
                        late_unit(*units.pop(0))
                    next_rows(2 * s + 1)
                    score_cols(3)
                    if last and units:
                        late_unit(*units.pop(0))

            step(0, first=True)
            for n in range(len(halves) - 2, len(halves)):
                pe.wait_ge(stacked[n], 16 * len(Q_SLOTS))
            with pe.Fori(1, LAST) as g:
                step(g)
            step(LAST, last=True)
            values(LAST, 15, st_score(LAST, 15, 3), None)
            turn_heads(1, SM_LAST["tail"] % 2, 2 * LAST + 2, SM_LAST["tail"] - 1)


def kernel(L0_attn_x, L0_attn_wq, L0_attn_bq, L0_attn_wk, L0_attn_bk, L0_attn_wv, L0_attn_bv,
           L0_ffn_W, L0_ffn_b, L0_ffn_A, L0_ffn_B, L0_ffn_p_scores):
    import concourse.bacc as bacc
    from concourse.bass_utils import run_bass_kernel_spmd

    def rows(a):
        a = np.asarray(a)
        a = a.reshape(*a.shape[:-1], -1, KV, D)[..., ROW_ORDER]
        return np.moveaxis(a, -1, -2).reshape(*a.shape[:-3], -1)

    def columns(a):
        own = a.reshape(-1, D, KV)
        partner = own.reshape(-1, D // 2, 2, KV)[:, :, ::-1].reshape(own.shape)
        return np.stack([own, partner], -1).reshape(-1, P, 2)

    inv_freq = np.float32(1.0) / np.float32(10000.0) ** (np.arange(0, D, 2, dtype=np.float32) / np.float32(D))
    ang = np.arange(S, dtype=np.float32)[:, None] * inv_freq[None, :]
    sign = np.array([-1.0 if d < D // 2 else 1.0 for d in ROW_ORDER], np.float32)
    pair = [d % (D // 2) for d in ROW_ORDER]
    cosT = np.repeat(np.cos(ang).T[pair], KV, axis=0)
    sinT = np.repeat(np.sin(ang).T[pair] * sign[:, None], KV, axis=0)

    f = {
        "x": np.asarray(L0_attn_x).reshape(S, E),
        "wq": rows(L0_attn_wq),
        "wk": rows(L0_attn_wk),
        "wv": np.asarray(L0_attn_wv),
        "biases": np.concatenate([columns(rows(L0_attn_bq)), columns(rows(L0_attn_bk))]).transpose(1, 0, 2),
        "bv": np.asarray(L0_attn_bv),
        "wT": np.asarray(L0_ffn_W).T,
        "b": np.asarray(L0_ffn_b),
        "A": np.asarray(L0_ffn_A).transpose(1, 0, 2).reshape(E, RANK),
        "B": np.asarray(L0_ffn_B).reshape(RANK, E),
        "p_sc": np.repeat(np.asarray(L0_ffn_p_scores), RANK // len(L0_ffn_p_scores))[:, None],
        "cosT": cosT.astype(np.float32),
        "sinT": sinT.astype(np.float32),
        "ident": np.eye(P, dtype=np.float32),
        "ones": np.ones((KM - KR, KV, S), np.float32).astype(mybir.dt.np(BF16)),
        "identb": np.eye(P, dtype=np.float32).astype(mybir.dt.np(BF16)),
    }
    nc = bacc.Bacc("TRN2", target_bir_lowering=False, num_devices=1)
    arrays = {f"in_{k}": np.ascontiguousarray(v) for k, v in f.items()}
    args = {k: nc.dram_tensor(f"in_{k}", v.shape, mybir.dt.from_np(v.dtype), kind="ExternalInput").ap()
            for k, v in ((k, arrays[f"in_{k}"]) for k in f)}
    out = nc.dram_tensor("out", (S, E), F32, kind="ExternalOutput").ap()
    build(nc, out=out, **args)
    r = run_bass_kernel_spmd(nc, [arrays], core_ids=[0])
    return r.results[0]["out"].reshape(1, S, E)
```
